# Optimizing a Trainium2 kernel written in Bass

```python
import numpy as np
import jax
import jax.numpy as jnp

def _softmax(x, axis=-1):
    return jax.nn.softmax(x, axis=axis)

def _gelu(x):
    return jax.nn.gelu(x, approximate=True)

def _silu(x):
    return jax.nn.silu(x)

def _sigmoid(x):
    return jax.nn.sigmoid(x)

def _layernorm(x, axis=-1, eps=1e-05):
    m = jnp.mean(x, axis=axis, keepdims=True)
    v = jnp.var(x, axis=axis, keepdims=True)
    return (x - m) / jnp.sqrt(v + eps)

def _scatter_add(tgt, idx, src, axis=0):
    return tgt.at[idx].add(src)

def _segment_sum(src, seg, n):
    return jax.ops.segment_sum(src, seg, n)
kernel_name = 'mk_prb_d1_jaxref_r4_aef46f'

def setup_inputs(seed: int=0):
    np.random.seed(seed)
    _w = jnp.asarray

    def _L0_attn_setup():
        import jax, jax.numpy as jnp
        import numpy as np
        import math
        D_MODEL = 256
        N_HEADS = 16
        BASE = 2500
        B, T = (8, 256)

        def hope_bias(pos_independent, T, d_model, n_heads, base):
            dim = d_model // 2
            pos = np.arange(dim, dtype=np.float64)
            freqs_np = 1.0 / base ** (pos / dim)
            active = int(np.sum(freqs_np * 2 * math.pi * T >= 1.0))
            active = min(active, dim - d_model // 4)
            freqs = jnp.asarray(freqs_np[:active], dtype=jnp.float32)
            d = jnp.arange(-(T - 1), T, dtype=jnp.float32)
            theta = d[:, None] * freqs[None, :]
            pv_high = jnp.cos(theta) + jnp.sin(theta)
            latter = dim - active
            pv_const = pos_independent[:latter].sum(axis=-1)
            pv = jnp.concatenate([pv_high, jnp.broadcast_to(pv_const[None, :], (2 * T - 1, latter))], axis=1)
            pairs_per_head = dim // n_heads
            per_head = pv.reshape(2 * T - 1, n_heads, pairs_per_head).sum(axis=-1)
            idx = jnp.arange(T)[:, None] - jnp.arange(T)[None, :] + (T - 1)
            return per_head[idx]
        key = jax.random.key(seed)
        ks = jax.random.split(key, 6)
        d = D_MODEL
        return {'x': jax.random.normal(ks[0], (B, T, d), dtype=jnp.float32), 'w_qkv': jax.random.normal(ks[1], (3 * d, d), dtype=jnp.float32) * 0.02, 'b_qkv': jnp.zeros((3 * d,), dtype=jnp.float32), 'w_proj': jax.random.normal(ks[2], (d, d), dtype=jnp.float32) * 0.02, 'b_proj': jnp.zeros((d,), dtype=jnp.float32), 'pos_independent': jax.random.normal(ks[3], (d // 4, 2), dtype=jnp.float32)}
    _L0_attn_in = _L0_attn_setup()

    def _L0_ffn_setup():
        import jax, jax.numpy as jnp
        import numpy as np
        FEATURES = 256
        D_IN = 256

        def fp8_gemm_optimized(x, input_scale, kernel, kernel_scale):
            s_in = input_scale[0]
            s_k = kernel_scale[0]
            x_q = (x.astype(jnp.float32) / s_in).astype(jnp.float8_e4m3fn)
            k_q = (kernel.astype(jnp.float32) / s_k).astype(jnp.float8_e4m3fn)
            y = jnp.dot(x_q.astype(jnp.float32), k_q.astype(jnp.float32), preferred_element_type=jnp.float32)
            return y * (s_in * s_k)
        key = jax.random.key(seed)
        kx, kk, kb = jax.random.split(key, 3)
        x = jax.random.normal(kx, (4, 2048, D_IN), dtype=jnp.float32)
        limit = np.sqrt(6.0 / (D_IN + FEATURES)).astype(np.float32)
        kernel = jax.random.uniform(kk, (D_IN, FEATURES), dtype=jnp.float32, minval=-limit, maxval=limit).astype(jnp.bfloat16)
        input_scale = jnp.ones((1,), dtype=jnp.float32)
        kernel_scale = jnp.ones((1,), dtype=jnp.float32)
        bias = jnp.zeros((FEATURES,), dtype=jnp.bfloat16)
        return {'x': x, 'kernel': kernel, 'input_scale': input_scale, 'kernel_scale': kernel_scale, 'bias': bias}
    _L0_ffn_in = _L0_ffn_setup()
    _d = {'L0_attn_x': _L0_attn_in['x'], 'L0_attn_w_qkv': _L0_attn_in['w_qkv'], 'L0_attn_b_qkv': _L0_attn_in['b_qkv'], 'L0_attn_w_proj': _L0_attn_in['w_proj'], 'L0_attn_b_proj': _L0_attn_in['b_proj'], 'L0_attn_pos_independent': _L0_attn_in['pos_independent'], 'L0_ffn_kernel': _L0_ffn_in['kernel'], 'L0_ffn_input_scale': _L0_ffn_in['input_scale'], 'L0_ffn_kernel_scale': _L0_ffn_in['kernel_scale'], 'L0_ffn_bias': _L0_ffn_in['bias']}
    _x0 = _d['L0_attn_x']
    _d['L0_attn_x'] = jax.random.normal(jax.random.fold_in(jax.random.key(seed), 1), (16, 512, 256), dtype=_x0.dtype)
    del _x0
    return _d

def reference(L0_attn_x, L0_attn_w_qkv, L0_attn_b_qkv, L0_attn_w_proj, L0_attn_b_proj, L0_attn_pos_independent, L0_ffn_kernel, L0_ffn_input_scale, L0_ffn_kernel_scale, L0_ffn_bias):

    def _L0_attn_ref(x, w_qkv, b_qkv, w_proj, b_proj, pos_independent):
        import jax, jax.numpy as jnp
        import numpy as np
        import math
        D_MODEL = 256
        N_HEADS = 16
        BASE = 2500
        B, T = (8, 256)

        def hope_bias(pos_independent, T, d_model, n_heads, base):
            dim = d_model // 2
            pos = np.arange(dim, dtype=np.float64)
            freqs_np = 1.0 / base ** (pos / dim)
            active = int(np.sum(freqs_np * 2 * math.pi * T >= 1.0))
            active = min(active, dim - d_model // 4)
            freqs = jnp.asarray(freqs_np[:active], dtype=jnp.float32)
            d = jnp.arange(-(T - 1), T, dtype=jnp.float32)
            theta = d[:, None] * freqs[None, :]
            pv_high = jnp.cos(theta) + jnp.sin(theta)
            latter = dim - active
            pv_const = pos_independent[:latter].sum(axis=-1)
            pv = jnp.concatenate([pv_high, jnp.broadcast_to(pv_const[None, :], (2 * T - 1, latter))], axis=1)
            pairs_per_head = dim // n_heads
            per_head = pv.reshape(2 * T - 1, n_heads, pairs_per_head).sum(axis=-1)
            idx = jnp.arange(T)[:, None] - jnp.arange(T)[None, :] + (T - 1)
            return per_head[idx]
        Bm, Tm, C = x.shape
        H = N_HEADS
        hd = C // H
        qkv = x @ w_qkv.T + b_qkv
        qkv = qkv.reshape(Bm, Tm, 3, H, hd).transpose(2, 0, 3, 1, 4)
        q, k, v = (qkv[0], qkv[1], qkv[2])
        att = jnp.einsum('bhqd,bhkd->bhqk', q, k) / jnp.sqrt(jnp.float32(hd))
        bias = hope_bias(pos_independent, Tm, C, H, BASE)
        att = att + bias.transpose(2, 0, 1)[None]
        causal = jnp.tril(jnp.ones((Tm, Tm), dtype=bool))
        att = jnp.where(causal[None, None], att, -jnp.inf)
        att = jax.nn.softmax(att, axis=-1)
        out = jnp.einsum('bhqk,bhkd->bhqd', att, v)
        out = out.transpose(0, 2, 1, 3).reshape(Bm, Tm, C)
        return out @ w_proj.T + b_proj

    def _L0_ffn_ref(x, kernel, input_scale, kernel_scale, bias):
        import jax, jax.numpy as jnp
        import numpy as np
        FEATURES = 256
        D_IN = 256

        def fp8_gemm_optimized(x, input_scale, kernel, kernel_scale):
            s_in = input_scale[0]
            s_k = kernel_scale[0]
            x_q = (x.astype(jnp.float32) / s_in).astype(jnp.float8_e4m3fn)
            k_q = (kernel.astype(jnp.float32) / s_k).astype(jnp.float8_e4m3fn)
            y = jnp.dot(x_q.astype(jnp.float32), k_q.astype(jnp.float32), preferred_element_type=jnp.float32)
            return y * (s_in * s_k)
        dtype = jnp.bfloat16
        x = x.astype(dtype)
        orig_shape = x.shape
        x2 = x.reshape(-1, x.shape[-1])
        y = fp8_gemm_optimized(x2, input_scale, kernel, kernel_scale)
        y = y.astype(dtype) + bias
        return y.reshape(orig_shape[:-1] + (FEATURES,))
    x = L0_attn_x
    xn = _layernorm(x, axis=-1)
    x = x + _L0_attn_ref(xn, L0_attn_w_qkv, L0_attn_b_qkv, L0_attn_w_proj, L0_attn_b_proj, L0_attn_pos_independent) + _L0_ffn_ref(xn, L0_ffn_kernel, L0_ffn_input_scale, L0_ffn_kernel_scale, L0_ffn_bias)
    return x

_drawn_inputs = setup_inputs


def setup_inputs(seed=0):
    import zlib

    import numpy as np

    out = dict(_drawn_inputs(seed))
    spreads = {'L0_attn_b_qkv': (0.0, 0.37), 'L0_attn_b_proj': (0.0, 0.1)}
    factors = {'L0_attn_pos_independent': 8.0}
    for name, (base, spread) in spreads.items():
        noise = np.random.default_rng([zlib.crc32(name.encode()), seed]).standard_normal(out[name].shape)
        drawn = base * np.exp(spread * noise) if base else spread * noise
        out[name] = jnp.asarray(drawn.astype(out[name].dtype))
    for name, factor in factors.items():
        out[name] = (out[name] * factor).astype(out[name].dtype)
    return out
```

```python
from contextlib import ExitStack

import numpy as np

import concourse.bass as bass
from concourse import mybir

P = 128
B, T, C = 16, 512, 256
H, HD = 16, 16
TT = T // P
CT = C // P
G = 4
HU = H // G
BASE = 2500
EPS = 1e-5
K_SCORE = 112
K_ALL = 114
SLOTS = 11
CHUNKS = 6
WJ = [T - P * j for j in range(TT)]
SLOT_PLAN = [(0, h, 1) for h in range(4)] + [(1, h, 1) for h in range(4)] + [(2, 0, 2), (2, 2, 2), (3, 0, 4)]
LAST_SLOT = [3, 7, 9, 10]
CHUNK_PLAN = [(3, 0, 2, 1), (3, 2, 2, 1), (2, 0, 2, 1), (2, 2, 2, 1), (1, 0, 4, 2), (0, 0, 4, 4)]
V_AT = [(0, 3), (0, 4)]
T_AT = [(0, 5), (0, 6)]
QK_AT = [(0, 8), (0, 10), (1, 4), (1, 6)]
FF_AT = [(2, 4), (2, 6)]
PJ_AT = [(3, 5), (3, 7)]
MASKED = -1.0e30
E4_LEAST = 2.0 ** -6
E4_MAGIC = 1.5 * 2.0 ** 20
E4_OVER = float(np.finfo(np.float32).max / np.float32(464.0))

F32 = mybir.dt.float32
F32R = mybir.dt.float32r
BF16 = mybir.dt.bfloat16
I32 = mybir.dt.int32
ALU = mybir.AluOpType
ACT = mybir.ActivationFunctionType
AX_X = mybir.AxisListType.X


def position_tables():
    dim = C // 2
    freqs = (1.0 / BASE ** (np.arange(dim, dtype=np.float64) / dim))[: dim - C // 4].astype(np.float32)
    angle = np.arange(T, dtype=np.float64)[None, :] * freqs.astype(np.float64)[:, None]
    c, s = np.cos(angle).reshape(8, 8, T), np.sin(angle).reshape(8, 8, T)
    q = np.concatenate([c, s], axis=1).reshape(P, T)
    k = np.concatenate([c - s, c + s], axis=1).reshape(P, T)
    return q.astype(np.float32), k.astype(np.float32)


def build(nc, x, w_qkv, b_qkv, w_proj, b_proj, pos, ffn_w, s_in, s_k, ffn_b, feat_q, feat_k, out):
    with ExitStack() as ctx:
        def sb(name, shape, dt):
            return ctx.enter_context(nc.sbuf_tensor(name, shape, dt))

        def ps(name, shape):
            return ctx.enter_context(nc.psum_tensor(name, shape, F32))

        def sem(name):
            return ctx.enter_context(nc.semaphore(name))

        STK = sb("stacks", [P, G, 2, HU, T], F32R)
        PROBS = sb("probs", [P, HU * sum(WJ)], F32)
        PJ = [PROBS[:, HU * sum(WJ[:j]):HU * sum(WJ[:j + 1])].rearrange("p (h n) -> p h n", h=HU) for j in range(TT)]
        X = sb("x_ring", [P, 4, TT, C], F32)
        XN = sb("xn", [P, TT, C], F32)
        XH = sb("xnT_hi", [P, CT, T], F32R)
        XL = sb("xnT_lo", [P, CT, T], F32R)
        QKP = sb("qk_parts", [P, 2, 4, 2, T], F32R)
        VA = sb("v_ones", [P, TT, H, 2, HD], F32)
        OT = sb("out_T", [P, 2, T], F32)
        AS = sb("attn", [P, 2, CT, T], F32)
        DEN = sb("denominators", [P, T // 8], F32)
        RDEN = sb("denominators_inv", [P, T // 8], F32)
        AH = sb("attn_hi", [P, CT, T], F32R)
        AL = sb("attn_lo", [P, CT, T], F32R)
        XB = sb("xnT_bf16", [P, CT, T], BF16)
        QZ = sb("quant_work", [P, 2, CT, T], F32)
        QT, QM = QZ[:, 0], QZ[:, 1]
        QE = XN[:, :, :].rearrange("p t c -> p (t c)").rearrange("p (a n) -> p a n", n=T)
        XQ = sb("xq", [P, CT, T], BF16)
        Y1 = XB[:, :, :].rearrange("p a n -> p (a n)").rearrange("p (t c) -> p t c", c=C)
        MX = sb("neg_max", [P, 2, HU, TT], F32)
        MP = sb("neg_max_parts", [P, 2, 2, HU * TT], F32)
        MTS = sb("neg_max_T", [2 * HU * TT, 2, P], F32R)
        ST6 = sb("bn_six", [P, TT, 6], F32)
        MV = sb("mean_var", [P, TT, 2], F32)
        VE = sb("var_eps", [P, TT], F32)
        RSTD = sb("rstd", [P, TT], F32)
        NH = sb("neg_half", [P, TT], F32)
        WH = sb("w_qkvT_hi", [P, CT, 3 * C], F32R)
        WL = sb("w_qkvT_lo", [P, CT, 3 * C], F32R)
        PH = sb("w_projT_hi", [P, CT, C], F32R)
        PL = sb("w_projT_lo", [P, CT, C], F32R)
        KQ = sb("ffn_w_q", [P, CT, C], BF16)
        IDF = sb("ident_f32", [P, P], F32)
        IDB = sb("ident_bf16", [P, P], BF16)
        CMT = sb("causal_mask_T", [P, P], BF16)
        BQ = sb("b_qk", [P, 4], F32)
        BV = sb("b_v", [P, C], F32)
        BP = sb("b_proj", [P, C], F32)
        BF = sb("b_ffn", [P, C], BF16)
        SC = sb("ffn_scales", [P, 5], F32)
        POS = sb("pos_col", [P, 1], F32)
        RB = XN[:, :, :].rearrange("p t c -> p (t c)").rearrange("p (a n) -> p a n", n=T)
        slabs = PROBS[:, :].rearrange("p (s n) -> p s n", n=T)
        w_raw = slabs[:, 0:3, :].rearrange("p s n -> p (s n)").rearrange("p (m c) -> p m c", c=C)
        wp_raw = AS[:, 0, 0, :].rearrange("p (b c) -> p b c", c=C)
        fq_raw, fk_raw = AS[:, 1, 0, :], AS[:, 1, 1, :]
        kern_raw = XQ[:, 0, :].rearrange("p (a c) -> p a c", c=C)
        x_tail = X[:, 2:4, :, :].rearrange("p s t c -> p (s t c)")[:, 0:3 * T]
        fq_parts = [slabs[:, 3:6, :].bitcast(F32R),
                    QZ[:, :, :, :].rearrange("p a b n -> p (a b) n")[:, 0:3, :].bitcast(F32R)]
        fk_parts = [slabs[:, 6:9, :].bitcast(F32R), x_tail.rearrange("p (r n) -> p r n", n=T).bitcast(F32R)]

        SB_ = [ps("score_a", [P, 2, 512]), ps("score_b", [P, 2, 512])]
        STB = [ps("scoreT_a", [P, 512]), ps("scoreT_b", [P, 512])]
        PVB = ps("pv", [P, 512])
        MB = ps("misc", [P, 512])

        w_loaded = sem("weights_loaded")
        small_loaded = sem("small_inputs_loaded")
        consts_made = sem("constants_made")
        ident_steps = sem("identity_steps")
        feat_raw = sem("features_loaded_raw")
        setup_T = sem("setup_transposed")
        setup_hi = sem("setup_hi_written")
        setup_lo = sem("setup_lo_written")
        setup_step = sem("setup_vector_steps")
        feat_parts = sem("feature_parts_made")
        feat_loaded = sem("features_in_stacks")
        kq_made = sem("ffn_weights_quantised")
        x_loaded = sem("x_loaded")
        bn_done = sem("bn_stats_done")
        mv_done = sem("mean_var_done")
        ve_done = sem("var_eps_done")
        rstd_done = sem("rstd_done")
        xn_ready = sem("xn_ready")
        t_ready = sem("xnT_in_psum")
        xb_ready = sem("xnT_bf16_written")
        xh_ready = sem("xnT_hi_written")
        xl_ready = sem("xnT_lo_written")
        qk_ready = sem("qk_in_psum")
        qh_ready = sem("qk_hi_written")
        ql_ready = sem("qk_lo_written")
        stack_loaded = [sem(f"stack{g}_loaded") for g in range(G)]
        max_loaded = [sem(f"max{g}_in_stack") for g in range(G)]
        s_ready = sem("scores_in_psum")
        max_done = sem("chunk_max_done")
        mh_done = sem("max_hi_done")
        mp_ready = sem("max_parts_ready")
        mt_ready = sem("max_T_in_psum")
        mts_ready = sem("max_T_written")
        st_ready = sem("scoresT_in_psum")
        exp_done = sem("exp_done")
        mask_done = sem("probs_masked")
        pv_done = sem("pv_done")
        ot_ready = sem("out_T_written")
        ot_stored = [sem(f"out_T{i}_regrouped") for i in range(2)]
        den_loaded = [sem(f"denominators{i}_regrouped") for i in range(2)]
        rc_ready = sem("denominators_inverted")
        rc_stored = sem("inverses_stored")
        rb_loaded = sem("inverses_spread")
        div_done = sem("attn_divided")
        ah_ready = sem("attn_hi_written")
        al_ready = sem("attn_lo_written")
        v_ready = sem("v_in_psum")
        va_ready = sem("v_written")
        qt_done = sem("quant_t_done")
        qz_done = sem("quant_over_done")
        qk_magic = sem("quant_guard_done")
        qe_done = sem("quant_exponent_done")
        qm_done = sem("quant_magic_done")
        qr_done = sem("quant_rounded")
        xq_ready = sem("xq_ready")
        ff_ready = sem("ffn_in_psum")
        y1_ready = sem("y1_written")
        y2_ready = sem("y2_written")
        xp_ready = sem("x_plus_bias")
        xy_ready = sem("x_plus_ffn")
        pj_ready = sem("proj_in_psum")
        out_ready = sem("out_written")
        out_stored = sem("out_stored")
        def part_copies(m):
            o = QKP[:, m // 2, :, m % 2, :]
            return (o[:, 0:2, :], o[:, 2:4, :]) if m % 2 == 0 else (o[:, 0:4:2, :], o[:, 1:4:2, :])

        def wait_alone(eng, always, *pairs):
            held = [(s, v if isinstance(v, int) else eng.compute_val(v)) for s, v in pairs]
            eng.wait_ge(*always)
            for s, v in held:
                eng.wait_ge(s, v)

        recips = nc.dram_tensor("recips", (H, T), F32, kind="Internal").ap()

        def attn_row(b):
            return AS[:, bass.ds(b % 2, 1), :, :].rearrange("p o a n -> p (o a) n")

        def x_slot(b):
            return X[:, bass.ds(b % 4, 1), :, :].rearrange("p o t c -> p (o t) c")

        block = ctx.enter_context(nc.Block())

        @block.sync
        def _(sp):
            def load_x(b):
                sp.dma_start(x_slot(b), x[bass.ds(b, 1), :, :].rearrange("o (t p) c -> p (o t) c", p=P)) \
                    .then_inc(x_loaded, 16)

            def load_stack(b, g):
                r0 = 64 * (g % 2)
                for h in range(HU):
                    rows = slice(r0 + 16 * h, r0 + 16 * h + 16)
                    for a in range(2):
                        sp.dma_start(STK[0:64, g, a, h, :].bitcast(F32),
                                     QKP[rows, g // 2, :, a, :].bitcast(F32)).then_inc(stack_loaded[g], 16)

            def load_max(b, g):
                sp.wait_ge(mts_ready, 4 * b + g + 1)
                sp.dma_start(STK[K_SCORE:K_ALL, g, 0, :, :].rearrange("p h n -> p (h n)").bitcast(F32),
                             MTS[:, g % 2, :].bitcast(F32)).then_inc(max_loaded[g], 16)

            def regroup(b, g, early):
                if g == 0 and not early:
                    wait_alone(sp, (w_loaded, 16), (al_ready, b), (rc_ready, b), (ot_ready, 4 * b + g + 1))
                else:
                    sp.wait_ge(ot_ready, 4 * b + g + 1)
                for i in range(HU):
                    r = 64 * (g % 2) + 16 * i
                    sp.dma_start(attn_row(b)[r:r + 16, g // 2, :],
                                 OT[32 * i:32 * i + HD, g % 2, :]).then_inc(ot_stored[g % 2], 16)
                sp.dma_start(DEN[32 * g:32 * g + 32, :], OT[HD:P:32, g % 2, :]).then_inc(den_loaded[g % 2], 16)

            def store_recips(b):
                wait_alone(sp, (w_loaded, 16), (rc_ready, b + 1), (rb_loaded, 32 * (b + 1)))
                sp.dma_start(recips.rearrange("h (e j) -> (h e) j", e=8), RDEN[:, :]).then_inc(rc_stored, 16)

            def spread_recips(b, last):
                if not last:
                    wait_alone(sp, (w_loaded, 16), (rc_stored, 16 * (b + 1)), (t_ready, 2 * (b + 3)))
                else:
                    sp.wait_ge(rc_stored, 16 * (b + 1))
                    sp.wait_ge(qm_done, B)
                    sp.wait_ge(div_done, b)
                for ct in range(CT):
                    src = recips[8 * ct:8 * ct + 8, :].unsqueeze(1).broadcast_to([8, HD, T])
                    sp.dma_start(RB[:, ct, :], src).then_inc(rb_loaded, 16)

            sp.sem_inc(out_stored, 16)
            sp.sem_inc(rb_loaded, 32)
            load_x(0)
            sp.dma_start(w_raw, w_qkv.rearrange("(m p) c -> p m c", p=P)).then_inc(w_loaded, 16)
            sp.dma_start(BQ[:, :], b_qkv[0:2 * C].rearrange("(m p) -> p m", p=P),
                         allow_slow_non_contiguous=True).then_inc(small_loaded, 16)
            sp.dma_start(SC[:, 0:1], s_in.partition_broadcast(P)).then_inc(small_loaded, 16)
            sp.dma_start(SC[:, 1:2], s_k.partition_broadcast(P)).then_inc(small_loaded, 16)
            sp.dma_start(BV[:, :], b_qkv[2 * C:3 * C].partition_broadcast(P)).then_inc(small_loaded, 16)
            sp.dma_start(BP[:, :], b_proj.partition_broadcast(P)).then_inc(small_loaded, 16)
            sp.dma_start(BF[:, :], ffn_b.partition_broadcast(P)).then_inc(small_loaded, 16)
            sp.dma_start(wp_raw, w_proj.rearrange("(m p) c -> p m c", p=P)).then_inc(small_loaded, 16)
            sp.dma_start(kern_raw, ffn_w.rearrange("(m p) c -> p m c", p=P)).then_inc(small_loaded, 16)
            sp.wait_ge(x_loaded, 16)
            load_x(1)
            sp.wait_ge(feat_parts, 4)
            for g in range(G):
                sp.dma_start(STK[K_SCORE:K_ALL, g, 1, :, :].bitcast(F32),
                             fq_parts[1][0:2, 0:1, :].bitcast(F32).broadcast_to([2, HU, T])) \
                    .then_inc(feat_loaded, 16)
            for h in range(H):
                r = 16 * (h % 8)
                sp.dma_start(STK[64:K_SCORE, h // HU, 0, h % HU, :].bitcast(F32),
                             fq_parts[h // 8][r:r + 16, :, :].bitcast(F32)) \
                    .then_inc(feat_loaded, 16)
            for g in range(3):
                sp.wait_ge(ql_ready, 2 if g < 2 else 4)
                load_stack(0, g)
            load_max(0, 0)

            def body(b, first, last, load):
                if load:
                    if not first:
                        sp.wait_ge(out_stored, 16 * b)
                    else:
                        sp.wait_ge(feat_loaded, 16 * (2 * H + G))
                    sp.wait_ge(x_loaded, 16 * (b + 2))
                    load_x(b + 2)
                if not first:
                    sp.wait_ge(st_ready, 44 * b)
                load_stack(b, 3)
                load_max(b, 1)
                if not first:
                    regroup(b - 1, 3, False)
                if not last:
                    wait_alone(sp, (w_loaded, 16), (st_ready, 44 * b + 11), (ql_ready, 4 * (b + 1) + 2))
                    load_stack(b + 1, 0)
                if not first:
                    store_recips(b - 1)
                load_max(b, 2)
                regroup(b, 0, first)
                if not first:
                    spread_recips(b - 1, last)
                if not last:
                    sp.wait_ge(st_ready, 44 * b + 22)
                    load_stack(b + 1, 1)
                load_max(b, 3)
                regroup(b, 1, first)
                if not last:
                    wait_alone(sp, (w_loaded, 16), (st_ready, 44 * b + 33), (ql_ready, 4 * (b + 1) + 4))
                    load_stack(b + 1, 2)
                    load_max(b + 1, 0)
                regroup(b, 2, first)
                if not first:
                    sp.wait_ge(out_ready, 2 * (b + 1))
                    sp.dma_start(out[bass.ds(b - 1, 1), :, :].rearrange("o (t p) c -> p (o t) c", p=P),
                                 x_slot(b + 3)).then_inc(out_stored, 16)

            body(0, True, False, True)
            with sp.Fori(1, B - 2) as b:
                body(b, False, False, True)
            body(B - 2, False, False, False)
            body(B - 1, False, True, False)
            regroup(B - 1, 3, False)
            store_recips(B - 1)
            spread_recips(B - 1, True)
            sp.wait_ge(out_ready, 2 * (B + 1))
            sp.dma_start(out[B - 1:B, :, :].rearrange("o (t p) c -> p (o t) c", p=P), x_slot(B - 1)) \
                .then_inc(out_stored, 16)
            sp.wait_ge(out_stored, 16 * (B + 1))

        @block.tensor
        def _(pe):
            mm = nc.tensor.matmul
            bank_read = [None]

            def misc(sem_after, value_after):
                if bank_read[0]:
                    pe.wait_ge(*bank_read[0])
                bank_read[0] = (sem_after, value_after)

            def split3(o, a, b_, n):
                (ah, al), (bh, bl) = a, b_
                for ct in range(CT):
                    for i, (l, r) in enumerate(((ah, bh), (ah, bl), (al, bh))):
                        last = mm(o, l(ct), r(ct), start=(ct == 0 and i == 0), stop=(ct == CT - 1 and i == 2))
                return last

            def job_T(b, ct):
                if ct == 0:
                    pe.wait_ge(xn_ready, b + 1)
                misc(xl_ready, 2 * b + ct + 1)
                for t in range(TT):
                    last = nc.tensor.transpose(MB[:, P * t:P * t + P], XN[:, t, P * ct:P * ct + P], IDF[:, :])
                last.then_inc(t_ready, 1)

            def job_QK(b, m):
                col = P * [0, 2, 1, 3][m]
                if m == 0:
                    pe.wait_ge(xl_ready, 2 * (b + 1))
                misc(ql_ready, 4 * b + m + 1)
                split3(MB[:, :], (lambda ct: WH[:, ct, col:col + P], lambda ct: WL[:, ct, col:col + P]),
                       (lambda ct: XH[:, ct, :], lambda ct: XL[:, ct, :]), T).then_inc(qk_ready, 1)

            def by_tokens(i, ah, al, bh, bl):
                for t in (2 * i, 2 * i + 1):
                    o = MB[:, C * (t % 2):C * (t % 2) + C]
                    last = split3(o, (lambda ct: ah[:, ct, P * t:P * t + P], lambda ct: al[:, ct, P * t:P * t + P]),
                                  (bh, bl), C)
                return last

            def job_V(b, i):
                misc(va_ready, 2 * b + i + 1)
                by_tokens(i, XH, XL, lambda ct: WH[:, ct, 2 * C:3 * C], lambda ct: WL[:, ct, 2 * C:3 * C]) \
                    .then_inc(v_ready, 1)

            def job_PJ(b, i):
                if i == 0:
                    pe.wait_ge(al_ready, b + 2)
                misc(out_ready, 2 * b + i + 3)
                by_tokens(i, AH, AL, lambda ct: PH[:, ct, :], lambda ct: PL[:, ct, :]).then_inc(pj_ready, 1)

            def job_FF(b, i):
                if i == 0:
                    pe.wait_ge(xq_ready, b + 1)
                    pe.wait_ge(kq_made, 1)
                misc(y1_ready, 2 * b + i + 1)
                for t in (2 * i, 2 * i + 1):
                    for ct in range(CT):
                        last = mm(MB[:, C * (t % 2):C * (t % 2) + C], XQ[:, ct, P * t:P * t + P], KQ[:, ct, :],
                                  start=(ct == 0), stop=(ct == CT - 1))
                last.then_inc(ff_ready, 1)

            def job_MT(b, g):
                pe.wait_ge(mp_ready, 4 * b + g + 1)
                misc(mts_ready, 4 * b + g + 1)
                nc.tensor.transpose(MB[0:2 * HU * TT, 0:P], MP[:, g % 2, :, :].rearrange("p a b -> p (a b)"),
                                    IDF[:, :]).then_inc(mt_ready, 1)

            def scores(b, g, c, early=False):
                qt, h0, nh, per = CHUNK_PLAN[c]
                w = P * (qt + 1)
                if c == 0:
                    pe.wait_ge(stack_loaded[g], 128 * (b + 1))
                if not (early and g == 0 and c < 2):
                    pe.wait_ge(max_done, 24 * b + 6 * g + c - 1)
                buf = SB_[c % 2]
                for i in range(nh):
                    h, o = h0 + i, w * (i % per)
                    mm(buf[:, i // per, o:o + w], STK[0:K_SCORE, g, 0, h, P * qt:P * qt + P],
                       STK[0:K_SCORE, g, 1, h, 0:w], start=True, stop=False)
                    last = mm(buf[:, i // per, o + w - P:o + w], CMT[:, :], IDB[:, :], start=False, stop=True)
                last.then_inc(s_ready, 1)

            def scores_T(b, g, k, first):
                j, h0, nh = SLOT_PLAN[k]
                w = WJ[j]
                if k == 0:
                    pe.wait_ge(max_loaded[g], 16 * (b + 1))
                if not (first and g == 0 and k < 2):
                    pe.wait_ge(exp_done, 44 * b + 11 * g + k - 1)
                bank = STB[(11 * g + k) % 2]
                for i in range(nh):
                    h = h0 + i
                    last = mm(bank[:, w * i:w * i + w], STK[0:K_ALL, g, 1, h, P * j:P * j + P],
                              STK[0:K_ALL, g, 0, h, P * j:T], start=True, stop=True)
                last.then_inc(st_ready, 1)

            def pv(b, g, j, first):
                pe.wait_ge(mask_done, 16 * b + 4 * g + j + 1)
                if j == 0:
                    if g == 0:
                        pe.wait_ge(va_ready, 2 * (b + 1))
                    if not (first and g == 0):
                        pe.wait_ge(ot_ready, 4 * b + g)
                for i in range(HU):
                    last = mm(PVB[32 * i:32 * i + 32, P * j:T],
                              VA[:, j, HU * g + i, :, :].rearrange("p a d -> p (a d)"),
                              PJ[j][:, i, :], start=(j == 0), stop=(j == TT - 1))
                last.then_inc(pv_done, 1)

            pe.sem_inc(pj_ready, 2)
            pe.wait_ge(ident_steps, 3)
            pe.wait_ge(w_loaded, 16)
            for n in range(4):
                ct, half = n // 2, n % 2
                for m in range(3):
                    last = nc.tensor.transpose(SB_[n // 2][:, n % 2, P * m:P * m + P],
                                               w_raw[:, 3 * half + m, P * ct:P * ct + P], IDF[:, :])
                last.then_inc(setup_T, 1)
            pe.wait_ge(small_loaded, 16 * 8)
            for ct in range(CT):
                for m in range(2):
                    last = nc.tensor.transpose(STB[ct][:, P * m:P * m + P], wp_raw[:, m, P * ct:P * ct + P], IDF[:, :])
                last.then_inc(setup_T, 1)
            for ct in range(CT):
                job_T(0, ct)
            pe.wait_ge(setup_lo, 6)
            for m in range(4):
                job_QK(0, m)
            pe.wait_ge(feat_loaded, 16 * (2 * H + G))
            pe.wait_ge(consts_made, 6)
            for c in range(CHUNKS):
                scores(0, 0, c, True)
            job_MT(0, 0)
            for c in range(CHUNKS):
                scores(0, 1, c, True)

            def body(b, first, last):
                if not first:
                    bank_read[0] = last_job(b)
                for g in range(G):
                    nb, ng = (b, g + 2) if g < 2 else (b + 1, g - 2)
                    ahead = not (last and g >= 2)
                    for k in range(SLOTS):
                        scores_T(b, g, k, first)
                        if k % 2 == 0 and ahead:
                            scores(nb, ng, k // 2)
                        pb, pg = (b, g - 1) if g else (b - 1, 3)
                        if k < 2 and not (first and g == 0):
                            pv(pb, pg, 2 + k, False)
                        if k == 2 and not (last and g == 3):
                            job_MT(*((b, g + 1) if g < 3 else (b + 1, 0)))
                        if (g, k) in V_AT:
                            job_V(b, V_AT.index((g, k)))
                        if (g, k) in T_AT and not last:
                            job_T(b + 1, T_AT.index((g, k)))
                        if (g, k) in QK_AT and not last:
                            job_QK(b + 1, QK_AT.index((g, k)))
                        if (g, k) in FF_AT:
                            job_FF(b, FF_AT.index((g, k)))
                        if (g, k) in PJ_AT and not first:
                            job_PJ(b - 1, PJ_AT.index((g, k)))
                        if k == 7:
                            pv(b, g, 0, first)
                        if k == 9:
                            pv(b, g, 1, first)

            body(0, True, False)
            pe.wait_ge(*bank_read[0])
            with pe.Fori(1, B - 1) as b:
                last_job = lambda b: (out_ready, 2 * b)
                body(b, False, False)
            body(B - 1, False, True)
            for j in (2, 3):
                pv(B - 1, 3, j, False)
            for i in range(2):
                job_PJ(B - 1, i)

        @block.scalar
        def _(act):
            A = nc.scalar.activation

            act.dma_start(fq_raw, feat_q).then_inc(feat_raw, 16)
            act.dma_start(fk_raw, feat_k).then_inc(feat_raw, 16)
            act.dma_start(POS[:, :], pos.rearrange("a b -> (a b)").rearrange("(p o) -> p o", o=1)) \
                .then_inc(feat_raw, 16)

            def T_evac(b, ct):
                act.wait_ge(t_ready, 2 * b + ct + 1)
                A(XB[:, ct, :], MB[:, :], ACT.Copy).then_inc(xb_ready, 1)
                A(XH[:, ct, :], MB[:, :], ACT.Copy).then_inc(xh_ready, 1)

            def QK_evac(b, m, first):
                act.wait_ge(qk_ready, 4 * b + m + 1)
                if not first:
                    for g in ((0, 1) if m < 2 else (2, 3)):
                        act.wait_ge(stack_loaded[g], 128 * b)
                bias = [0, 2, 1, 3][m]
                A(part_copies(m)[0], MB[:, :].unsqueeze(1).broadcast_to([P, 2, T]), ACT.Identity,
                  bias=BQ[:, bias:bias + 1]).then_inc(qh_ready, 1)

            for n in range(4):
                ct, half = n // 2, n % 2
                act.wait_ge(setup_T, n + 1)
                src = SB_[n // 2][:, n % 2, 0:3 * P]
                if half == 0:
                    A(WH[:, ct, 0:C], src[:, 0:C], ACT.Copy, scale=HD ** -0.5)
                    A(WH[:, ct, C:3 * P], src[:, C:3 * P], ACT.Copy).then_inc(setup_hi, 1)
                else:
                    A(WH[:, ct, 3 * P:3 * C], src, ACT.Copy).then_inc(setup_hi, 1)
            for ct in range(CT):
                act.wait_ge(setup_T, 5 + ct)
                A(PH[:, ct, :], STB[ct][:, 0:C], ACT.Copy).then_inc(setup_hi, 1)
            act.wait_ge(feat_parts, 4)
            for h in range(H):
                r = 16 * (h % 8)
                act.dma_start(STK[64:K_SCORE, h // HU, 1, h % HU, :].bitcast(F32),
                              fk_parts[h // 8][r:r + 16, :, :].bitcast(F32)) \
                    .then_inc(feat_loaded, 16)
            for ct in range(CT):
                T_evac(0, ct)
            act.wait_ge(setup_step, 3)
            for m in range(4):
                QK_evac(0, m, True)

            def out_T(b, g, skip_wait):
                act.wait_ge(pv_done, 16 * b + 4 * g + 4)
                if not skip_wait:
                    act.wait_ge(ot_stored[g % 2], 64 * (2 * b + g // 2))
                    act.wait_ge(den_loaded[g % 2], 16 * (2 * b + g // 2))
                A(OT[:, g % 2, :], PVB[:, :], ACT.Copy).then_inc(ot_ready, 1)

            def body(b, first, last):
                for g in range(G):
                    for k in range(SLOTS):
                        j, h0, nh = SLOT_PLAN[k]
                        act.wait_ge(st_ready, 44 * b + 11 * g + k + 1)
                        if k in (0, 4, 8, 10) and not (first and g == 0):
                            act.wait_ge(pv_done, 16 * b + 4 * g + j - 3)
                        A(PJ[j][:, h0:h0 + nh, :], STB[(11 * g + k) % 2][:, 0:nh * WJ[j]]
                          .rearrange("p (h n) -> p h n", h=nh), ACT.Exp).then_inc(exp_done, 1)
                        pb, pg = (b, g - 1) if g else (b - 1, 3)
                        if not (first and g == 0):
                            if k == 2:
                                out_T(pb, pg, first and pg < 2)
                        if (g, k) in T_AT and not last:
                            i = T_AT.index((g, k))
                            if i == 0 and not first:
                                act.wait_ge(xy_ready, b)
                            T_evac(b + 1, i)
                        if (g, k) in QK_AT and not last:
                            QK_evac(b + 1, QK_AT.index((g, k)), False)
                        if (g, k) in FF_AT:
                            i = FF_AT.index((g, k))
                            act.wait_ge(ff_ready, 2 * b + i + 1)
                            if i == 0 and not last:
                                act.wait_ge(qz_done, b + 2)
                            A(Y1[:, 2 * i:2 * i + 2, :], MB[:, :].rearrange("p (t c) -> p t c", c=C),
                              ACT.Identity, scale=SC[:, 3:4]).then_inc(y1_ready, 1)

            body(0, True, False)
            with act.Fori(1, B - 1) as b:
                body(b, False, False)
            body(B - 1, False, True)
            out_T(B - 1, 3, False)

        @block.vector
        def _(dve):
            V = nc.vector

            def stats(b):
                dve.wait_ge(x_loaded, 16 * (b + 1))
                for t in range(TT):
                    V.bn_stats(ST6[:, t, :], x_slot(b)[:, t, :]).then_inc(bn_done, 1)
                for t in range(TT):
                    wait_alone(dve, (small_loaded, 16 * 8), (bn_done, 4 * b + t + 1))
                    V.bn_aggr(MV[:, t, :], ST6[:, t, :]).then_inc(mv_done, 1)
                dve.wait_ge(mv_done, 4 * b + 4)
                V.tensor_scalar(VE[:, :], MV[:, :, 1], EPS, None, ALU.add).then_inc(ve_done, 1)

            def normalise(b):
                dve.wait_ge(rstd_done, b + 1)
                dve.wait_ge(t_ready, 2 * b)
                dve.wait_ge(qm_done, b)
                for t in range(TT):
                    ins = V.tensor_scalar(XN[:, t, :], x_slot(b)[:, t, :], MV[:, t, 0:1], RSTD[:, t:t + 1],
                                          ALU.subtract, ALU.mult)
                ins.then_inc(xn_ready, 1)

            def T_lo(b, ct):
                dve.wait_ge(xh_ready, 2 * b + ct + 1)
                V.tensor_tensor(XL[:, ct, :], MB[:, :], XH[:, ct, :].bitcast(F32), ALU.subtract) \
                    .then_inc(xl_ready, 1)

            def QK_lo(b, m):
                bias = [0, 2, 1, 3][m]
                dve.wait_ge(qh_ready, 4 * b + m + 1)
                hi, lo = part_copies(m)
                V.scalar_tensor_tensor(out=lo, in0=MB[:, :].unsqueeze(1).broadcast_to([P, 2, T]),
                                       scalar=BQ[:, bias:bias + 1], in1=hi.bitcast(F32),
                                       op0=ALU.add, op1=ALU.subtract) \
                    .then_inc(ql_ready, 1)

            def chunk_max(b, g, c):
                qt, h0, nh, per = CHUNK_PLAN[c]
                w = P * (qt + 1)
                buf = SB_[c % 2]
                src = (buf[:, :, 0:w] if per == 1 else buf[:, :, :].rearrange("p b (h w) -> p (b h) w", w=w)
                       if per == 2 else buf[:, 0, :].rearrange("p (h w) -> p h w", w=w))
                dve.wait_ge(s_ready, 24 * b + 6 * g + c + 1)
                V.tensor_reduce(MX[:, g % 2, h0:h0 + nh, qt], src, AX_X, ALU.max, negate=True) \
                    .then_inc(max_done, 1)

            def max_parts(b, g):
                p = g % 2
                mx = MX[:, p, :, :].rearrange("p h t -> p (h t)")
                dve.wait_ge(max_done, 24 * b + 6 * g + 6)
                V.tensor_copy(MP[:, p, 0, :].bitcast(F32R), mx).then_inc(mh_done, 1)
                dve.wait_ge(mh_done, 4 * b + g + 1)
                V.tensor_tensor(MP[:, p, 1, :], mx, MP[:, p, 0, :], ALU.subtract).then_inc(mp_ready, 1)

            def max_T(b, g):
                dve.wait_ge(mt_ready, 4 * b + g + 1)
                V.tensor_copy(MTS[:, g % 2, :], MB[0:2 * HU * TT, 0:P]).then_inc(mts_ready, 1)

            def v_evac(b, i, first):
                dve.wait_ge(v_ready, 2 * b + i + 1)
                if i == 0 and not first:
                    dve.wait_ge(pv_done, 16 * b)
                V.tensor_tensor(VA[:, 2 * i:2 * i + 2, :, 0, :],
                                MB[:, :].rearrange("p (t h d) -> p t h d", h=H, d=HD),
                                BV[:, :].rearrange("p (h d) -> p h d", d=HD).unsqueeze(1).broadcast_to([P, 2, H, HD]),
                                ALU.add).then_inc(va_ready, 1)

            def invert(b):
                for i in range(2):
                    dve.wait_ge(den_loaded[i], 32 * (b + 1))
                V.reciprocal(RDEN[:, :], DEN[:, :]).then_inc(rc_ready, 1)

            def divide(b):
                dve.wait_ge(rb_loaded, 32 * (b + 2))
                for i in range(2):
                    dve.wait_ge(ot_stored[i], 128 * (b + 1))
                V.tensor_tensor(attn_row(b), attn_row(b), RB, ALU.mult).then_inc(div_done, 1)
                wait_alone(dve, (small_loaded, 16 * 8), (pj_ready, 2 * (b + 1)), (div_done, b + 1))
                V.tensor_scalar(AH[:, :, :], attn_row(b), 1.0, None, ALU.mult).then_inc(ah_ready, 1)

            def result(b, i):
                dve.wait_ge(pj_ready, 2 * b + i + 3)
                dve.wait_ge(xy_ready, b + 1)
                xs = x_slot(b + 4)[:, 2 * i:2 * i + 2, :]
                V.tensor_tensor(xs, MB[:, :].rearrange("p (t c) -> p t c", c=C), xs, ALU.add) \
                    .then_inc(out_ready, 1)

            def quant_magic(b):
                dve.wait_ge(qk_magic, b + 1)
                V.tensor_scalar(QE.bitcast(I32), QT.bitcast(I32), 0x7F800000, None, ALU.bitwise_and) \
                    .then_inc(qe_done, 1)
                dve.wait_ge(qe_done, b + 1)
                V.scalar_tensor_tensor(out=QM, in0=QE, scalar=E4_LEAST, in1=QM, op0=ALU.max, op1=ALU.mult) \
                    .then_inc(qm_done, 1)

            step = [0]

            def then(ins):
                step[0] += 1
                ins.then_inc(setup_step, 1)
                dve.wait_ge(setup_step, step[0])

            dve.sem_inc(out_ready, 2)
            dve.wait_ge(small_loaded, 16 * 8)
            then(V.tensor_scalar(BQ[:, 0:2], BQ[:, 0:2], HD ** -0.5, None, ALU.mult))
            V.reciprocal(SC[:, 4:5], SC[:, 1:2])
            then(V.reciprocal(SC[:, 2:3], SC[:, 0:1]))
            then(V.tensor_tensor(SC[:, 3:4], SC[:, 0:1], SC[:, 1:2], ALU.mult))
            dve.wait_ge(feat_raw, 48)
            V.memset(fq_parts[1][:, 0:2, :].bitcast(F32), 1.0)
            V.memset(fq_parts[1][:, 2:3, :].bitcast(F32), 0.0).then_inc(feat_parts, 1)
            for raw, parts, order in ((fq_raw, fq_parts[0], (0, 1, 2)), (fk_raw, fk_parts[0], (0, 2, 1)),
                                      (POS[:, 0:1].broadcast_to([P, T]), fk_parts[1], (0, 2, 1))):
                V.tensor_copy(parts[:, order[1], :], raw)
                then(V.tensor_copy(parts[:, order[0], :], raw))
                V.tensor_tensor(parts[:, order[2], :], raw, parts[:, order[0], :].bitcast(F32), ALU.subtract) \
                    .then_inc(feat_parts, 1)
            for n in range(4):
                ct, half = n // 2, n % 2
                src = SB_[n // 2][:, n % 2, 0:3 * P]
                dve.wait_ge(setup_hi, n + 1)
                if half == 0:
                    V.scalar_tensor_tensor(out=WL[:, ct, 0:C], in0=src[:, 0:C], scalar=HD ** -0.5,
                                           in1=WH[:, ct, 0:C].bitcast(F32), op0=ALU.mult, op1=ALU.subtract)
                    V.tensor_tensor(WL[:, ct, C:3 * P], src[:, C:3 * P], WH[:, ct, C:3 * P].bitcast(F32),
                                    ALU.subtract).then_inc(setup_lo, 1)
                else:
                    V.tensor_tensor(WL[:, ct, 3 * P:3 * C], src, WH[:, ct, 3 * P:3 * C].bitcast(F32),
                                    ALU.subtract).then_inc(setup_lo, 1)
            for ct in range(CT):
                dve.wait_ge(setup_hi, 5 + ct)
                V.tensor_tensor(PL[:, ct, :], STB[ct][:, 0:C], PH[:, ct, :].bitcast(F32), ALU.subtract) \
                    .then_inc(setup_lo, 1)
            stats(0)
            dve.wait_ge(rstd_done, 1)
            for t in range(TT):
                ins = V.tensor_scalar(XN[:, t, :], x_slot(0)[:, t, :], MV[:, t, 0:1], RSTD[:, t:t + 1],
                                      ALU.subtract, ALU.mult)
            ins.then_inc(xn_ready, 1)
            for ct in range(CT):
                T_lo(0, ct)
            for m in range(4):
                QK_lo(0, m)
            dve.wait_ge(feat_loaded, 16 * (2 * H + G))
            kt, ke, km = QZ[:, 0, 0, :], QZ[:, 0, 1, :], QZ[:, 1, 0, :]
            kr = XQ[:, 0, :]
            then(V.tensor_scalar(kt, kr, SC[:, 4:5], None, ALU.mult))
            then(V.tensor_scalar(km, kt, E4_OVER, None, ALU.mult))
            then(V.tensor_scalar(km, km, 0.0, E4_MAGIC, ALU.mult, ALU.add))
            then(V.tensor_scalar(ke.bitcast(I32), kt.bitcast(I32), 0x7F800000, None, ALU.bitwise_and))
            then(V.scalar_tensor_tensor(out=km, in0=ke, scalar=E4_LEAST, in1=km, op0=ALU.max, op1=ALU.mult))
            then(V.tensor_tensor(kt, kt, km, ALU.add))
            V.tensor_tensor(KQ[:, :, :].rearrange("p a c -> p (a c)"), kt, km, ALU.subtract).then_inc(kq_made, 1)
            for c in range(CHUNKS):
                chunk_max(0, 0, c)
            max_parts(0, 0)
            max_T(0, 0)
            for c in range(CHUNKS):
                chunk_max(0, 1, c)
            max_parts(0, 1)
            quant_magic(0)
            stats(1)
            normalise(1)

            def body(b, first, last, more):
                for g in range(G):
                    nb, ng = (b, g + 2) if g < 2 else (b + 1, g - 2)
                    ahead = not (last and g >= 2)
                    for k in range(SLOTS):
                        if k % 2 == 0 and ahead:
                            chunk_max(nb, ng, k // 2)
                        if k == 2 and not (last and g == 3):
                            max_T(*((b, g + 1) if g < 3 else (b + 1, 0)))
                        if (g, k) in V_AT:
                            v_evac(b, V_AT.index((g, k)), first)
                        if (g, k) in T_AT and not last:
                            T_lo(b + 1, T_AT.index((g, k)))
                        if (g, k) in QK_AT and not last:
                            QK_lo(b + 1, QK_AT.index((g, k)))
                        if (g, k) in PJ_AT and not first:
                            result(b - 1, PJ_AT.index((g, k)))
                        if (g, k) == (1, 1) and not first:
                            invert(b - 1)
                        if (g, k) == (2, 2) and not first:
                            divide(b - 1)
                        if (g, k) == (2, 6) and more:
                            stats(b + 2)
                        if (g, k) == (2, 8) and not last:
                            quant_magic(b + 1)
                        if (g, k) == (3, 9) and more:
                            normalise(b + 2)
                    if ahead:
                        max_parts(nb, ng)

            body(0, True, False, True)
            with dve.Fori(1, B - 2) as b:
                body(b, False, False, True)
            body(B - 2, False, False, False)
            body(B - 1, False, True, False)
            invert(B - 1)
            divide(B - 1)
            for i in range(2):
                result(B - 1, i)

        @block.gpsimd
        def _(pool):
            GP = nc.gpsimd

            def rstd(b):
                pool.wait_ge(ve_done, b + 1)
                GP.tensor_tensor(RSTD[:, :], VE[:, :], NH[:, :], ALU.pow).then_inc(rstd_done, 1)

            def quant_scale(b):
                wait_alone(pool, (ident_steps, 3), (xb_ready, 2 * (b + 1)))
                GP.tensor_scalar(QT, XB[:, :, :], SC[:, 2:3], 1.0, ALU.mult, ALU.mult).then_inc(qt_done, 1)
                GP.tensor_scalar(QM, XB[:, :, :], SC[:, 2:3], E4_OVER, ALU.mult, ALU.mult).then_inc(qz_done, 1)
                wait_alone(pool, (ident_steps, 3), (qz_done, b + 1))
                GP.tensor_scalar(QM, QM, 0.0, E4_MAGIC, ALU.mult, ALU.add).then_inc(qk_magic, 1)

            def quant_round(b):
                pool.wait_ge(qm_done, b + 1)
                GP.tensor_tensor(QT, QT, QM, ALU.add).then_inc(qr_done, 1)

            def quant_write(b):
                pool.wait_ge(qr_done, b + 1)
                pool.wait_ge(ff_ready, 2 * b)
                GP.tensor_tensor(XQ[:, :, :], QT, QM, ALU.subtract).then_inc(xq_ready, 1)

            def mask(b, g, j):
                wait_alone(pool, (ident_steps, 3), (exp_done, 44 * b + 11 * g + LAST_SLOT[j] + 1))
                d = PJ[j][:, :, 0:P]
                GP.affine_select(out=d, in_=d, compare_op=ALU.is_ge, fill=0.0, base=0,
                                 pattern=[[0, HU], [1, P]], channel_multiplier=-1).then_inc(mask_done, 1)

            def ffn_bias(b):
                pool.wait_ge(y1_ready, 2 * (b + 1))
                GP.tensor_tensor(Y1[:, :, :], Y1[:, :, :], BF[:, :].unsqueeze(1).broadcast_to([P, TT, C]),
                                 ALU.add).then_inc(y2_ready, 1)

            def add_ffn(b):
                pool.wait_ge(y2_ready, b + 1)
                pool.wait_ge(xp_ready, b + 1)
                xs = x_slot(b + 4)
                GP.tensor_tensor(xs, xs, Y1[:, :, :], ALU.add).then_inc(xy_ready, 1)

            def add_bias(b):
                pool.wait_ge(xn_ready, b + 1)
                xs = x_slot(b)
                GP.tensor_tensor(xs, xs, BP[:, :].unsqueeze(1).broadcast_to([P, TT, C]), ALU.add) \
                    .then_inc(xp_ready, 1)

            def attn_parts(b):
                pool.wait_ge(ah_ready, b + 1)
                GP.tensor_tensor(AL[:, :, :], attn_row(b), AH[:, :, :].bitcast(F32), ALU.subtract) \
                    .then_inc(al_ready, 1)

            pool.sem_inc(al_ready, 1)
            GP.memset(IDF[:, :], 0.0).then_inc(ident_steps, 1)
            pool.wait_ge(ident_steps, 1)
            GP.affine_select(out=IDF[:, :], in_=IDF[:, :], compare_op=ALU.not_equal, fill=1.0, base=0,
                             pattern=[[-1, P]], channel_multiplier=1).then_inc(ident_steps, 2)
            GP.memset(IDB[:, :], 0.0).then_inc(consts_made, 1)
            GP.memset(CMT[:, :], 0.0).then_inc(consts_made, 1)
            pool.wait_ge(consts_made, 2)
            GP.affine_select(out=IDB[:, :], in_=IDB[:, :], compare_op=ALU.not_equal, fill=1.0, base=0,
                             pattern=[[-1, P]], channel_multiplier=1).then_inc(consts_made, 1)
            GP.affine_select(out=CMT[:, :], in_=CMT[:, :], compare_op=ALU.is_ge, fill=MASKED, base=0,
                             pattern=[[1, P]], channel_multiplier=-1).then_inc(consts_made, 1)
            GP.memset(NH[:, :], -0.5).then_inc(consts_made, 1)
            pool.wait_ge(consts_made, 5)
            rstd(0)
            GP.memset(VA[:, :, :, :, :].rearrange("p t h a d -> p (t h a d)"), 1.0).then_inc(consts_made, 1)
            pool.wait_ge(kq_made, 1)
            quant_scale(0)
            quant_round(0)
            quant_write(0)
            rstd(1)

            def body(b, first, last, more):
                for g in range(G):
                    if g == 0 and not first:
                        ffn_bias(b - 1)
                        add_ffn(b - 1)
                    if g == 1 and not last:
                        quant_scale(b + 1)
                    if g == 3 and not last:
                        quant_round(b + 1)
                    if g == 3 and more:
                        rstd(b + 2)
                    mask(b, g, 0)
                    if g == 1:
                        add_bias(b)
                    if g == 2 and not first:
                        attn_parts(b - 1)
                    if g == 3 and not last:
                        quant_write(b + 1)
                    for j in (1, 2, 3):
                        mask(b, g, j)

            body(0, True, False, True)
            with pool.Fori(1, B - 2) as b:
                body(b, False, False, True)
            body(B - 2, False, False, False)
            body(B - 1, False, True, False)
            ffn_bias(B - 1)
            add_ffn(B - 1)
            attn_parts(B - 1)

    return nc


_INS = ["L0_attn_x", "L0_attn_w_qkv", "L0_attn_b_qkv", "L0_attn_w_proj", "L0_attn_b_proj",
        "L0_attn_pos_independent", "L0_ffn_kernel", "L0_ffn_input_scale", "L0_ffn_kernel_scale", "L0_ffn_bias"]


def kernel(**inputs):
    import numpy as _np
    import concourse.bacc as _bacc
    from concourse import mybir as _mybir
    from concourse.bass_utils import run_bass_kernel_spmd as _run

    nc = _bacc.Bacc("TRN2", target_bir_lowering=False, num_devices=1)
    arrays, args = {}, []

    def give(name, a):
        arrays[name] = a
        args.append(nc.dram_tensor(name, a.shape, _mybir.dt.from_np(a.dtype), kind="ExternalInput").ap())

    for name in _INS:
        give(f"in_{name}", _np.ascontiguousarray(inputs[name]))
    for name, table in zip(("feature_q", "feature_k"), position_tables()):
        give(name, table)
    args.append(nc.dram_tensor("out", (B, T, C), F32, kind="ExternalOutput").ap())
    build(nc, *args)
    r = _run(nc, [arrays], core_ids=[0])
    return r.results[0]["out"]
```

```python
from contextlib import ExitStack

import numpy as np

import concourse.bass as bass
from concourse import mybir

P = 128
B, T, C = 16, 512, 256
H, HD = 16, 16
TT = T // P
CT = C // P
G = 4
HU = H // G
BASE = 2500
EPS = 1e-5
K_SCORE = 112
K_ALL = 114
SLOTS = 11
CHUNKS = 6
WJ = [T - P * j for j in range(TT)]
SLOT_PLAN = [(0, h, 1) for h in range(4)] + [(1, h, 1) for h in range(4)] + [(2, 0, 2), (2, 2, 2), (3, 0, 4)]
LAST_SLOT = [3, 7, 9, 10]
CHUNK_PLAN = [(3, 0, 2, 1), (3, 2, 2, 1), (2, 0, 2, 1), (2, 2, 2, 1), (1, 0, 4, 2), (0, 0, 4, 4)]
V_AT = [(0, 0), (0, 3)]
T_AT = [(0, 6), (0, 8)]
QK_AT = [(0, 10), (1, 5), (1, 6), (1, 8)]
FF_AT = [(2, 1), (2, 9)]
PJ_AT = [(3, 5), (3, 7)]
MT_AT = [4, 1, 3, 0]
INVERT_AT, DIVIDE_AT, STATS_AT, MAGIC_AT, NORM_AT = (1, 1), (2, 2), (2, 6), (3, 0), (3, 9)
PV_AT = [7, 10, 0, 1]
OUT_AT = 1
MASKED = -1.0e30
E4_LEAST = 2.0 ** -6
E4_MAGIC = 1.5 * 2.0 ** 20
E4_OVER = float(np.finfo(np.float32).max / np.float32(464.0))

F32 = mybir.dt.float32
F32R = mybir.dt.float32r
BF16 = mybir.dt.bfloat16
I32 = mybir.dt.int32
ALU = mybir.AluOpType
ACT = mybir.ActivationFunctionType
AX_X = mybir.AxisListType.X


def position_tables():
    dim = C // 2
    freqs = (1.0 / BASE ** (np.arange(dim, dtype=np.float64) / dim))[: dim - C // 4].astype(np.float32)
    angle = np.arange(T, dtype=np.float64)[None, :] * freqs.astype(np.float64)[:, None]
    c, s = np.cos(angle).reshape(8, 8, T), np.sin(angle).reshape(8, 8, T)
    q = np.concatenate([c, s], axis=1).reshape(P, T)
    k = np.concatenate([c - s, c + s], axis=1).reshape(P, T)
    return q.astype(np.float32), k.astype(np.float32)


def build(nc, x, w_qkv, b_qkv, w_proj, b_proj, pos, ffn_w, s_in, s_k, ffn_b, feat_q, feat_k, out):
    with ExitStack() as ctx:
        def sb(name, shape, dt):
            return ctx.enter_context(nc.sbuf_tensor(name, shape, dt))

        def ps(name, shape):
            return ctx.enter_context(nc.psum_tensor(name, shape, F32))

        def sem(name):
            return ctx.enter_context(nc.semaphore(name))

        STK = sb("stacks", [P, G, 2, HU, T], F32R)
        PROBS = sb("probs", [P, HU * sum(WJ)], F32)
        PJ = [PROBS[:, HU * sum(WJ[:j]):HU * sum(WJ[:j + 1])].rearrange("p (h n) -> p h n", h=HU) for j in range(TT)]
        X = sb("x_ring", [P, 4, TT, C], F32)
        XN = sb("xn", [P, TT, C], F32)
        XH = sb("xnT_hi", [P, CT, T], F32R)
        XL = sb("xnT_lo", [P, CT, T], F32R)
        QKP = sb("qk_parts", [P, 2, 4, 2, T], F32R)
        VA = sb("v_ones", [P, TT, H, 2, HD], F32)
        OT = sb("out_T", [P, 2, T], F32)
        AS = sb("attn", [P, 2, CT, T], F32)
        DEN = sb("denominators", [P, T // 8], F32)
        RDEN = sb("denominators_inv", [P, T // 8], F32)
        AH = sb("attn_hi", [P, CT, T], F32R)
        AL = sb("attn_lo", [P, CT, T], F32R)
        XB = sb("xnT_bf16", [P, CT, T], BF16)
        QZ = sb("quant_work", [P, 2, CT, T], F32)
        QT, QM = QZ[:, 0], QZ[:, 1]
        QE = XN[:, :, :].rearrange("p t c -> p (t c)").rearrange("p (a n) -> p a n", n=T)
        XQ = sb("xq", [P, CT, T], BF16)
        Y1 = XB[:, :, :].rearrange("p a n -> p (a n)").rearrange("p (t c) -> p t c", c=C)
        MX = sb("neg_max", [P, 2, HU, TT], F32)
        MP = sb("neg_max_parts", [P, 2, 2, HU * TT], F32)
        MTS = sb("neg_max_T", [2 * HU * TT, 2, P], F32R)
        ST6 = sb("bn_six", [P, TT, 6], F32)
        MV = sb("mean_var", [P, TT, 2], F32)
        VE = sb("var_eps", [P, TT], F32)
        RSTD = sb("rstd", [P, TT], F32)
        NH = sb("neg_half", [P, TT], F32)
        WH = sb("w_qkvT_hi", [P, CT, 3 * C], F32R)
        WL = sb("w_qkvT_lo", [P, CT, 3 * C], F32R)
        PH = sb("w_projT_hi", [P, CT, C], F32R)
        PL = sb("w_projT_lo", [P, CT, C], F32R)
        KQ = sb("ffn_w_q", [P, CT, C], BF16)
        IDF = sb("ident_f32", [P, P], F32)
        IDB = sb("ident_bf16", [P, P], BF16)
        CMT = sb("causal_mask_T", [P, P], BF16)
        BQ = sb("b_qk", [P, 4], F32)
        BV = sb("b_v", [P, C], F32)
        BP = sb("b_proj", [P, C], F32)
        BF = sb("b_ffn", [P, C], BF16)
        SC = sb("ffn_scales", [P, 5], F32)
        POS = sb("pos_col", [P, 1], F32)
        RB = QE
        slabs = PROBS[:, :].rearrange("p (s n) -> p s n", n=T)
        w_raw = slabs[:, 0:3, :].rearrange("p s n -> p (s n)").rearrange("p (m c) -> p m c", c=C)
        wp_raw = AS[:, 0, 0, :].rearrange("p (b c) -> p b c", c=C)
        fq_raw, fk_raw = AS[:, 1, 0, :], AS[:, 1, 1, :]
        kern_raw = XQ[:, 0, :].rearrange("p (a c) -> p a c", c=C)
        x_tail = X[:, 2:4, :, :].rearrange("p s t c -> p (s t c)")[:, 0:3 * T]
        fq_parts = slabs[:, 3:6, :].bitcast(F32R)
        fk_parts = [slabs[:, 6:9, :].bitcast(F32R), x_tail.rearrange("p (r n) -> p r n", n=T).bitcast(F32R)]

        SB_ = [ps("score_a", [P, 2, 512]), ps("score_b", [P, 2, 512])]
        STB = [ps("scoreT_a", [P, 512]), ps("scoreT_b", [P, 512])]
        PVB = ps("pv", [P, 512])
        MB = ps("misc", [P, 512])

        w_loaded = sem("weights_loaded")
        small_loaded = sem("small_inputs_loaded")
        consts_made = sem("constants_made")
        ident_steps = sem("identity_steps")
        feat_raw = sem("features_loaded_raw")
        setup_T = sem("setup_transposed")
        setup_hi = sem("setup_hi_written")
        setup_lo = sem("setup_lo_written")
        setup_step = sem("setup_vector_steps")
        feat_parts = sem("feature_parts_made")
        ones_made = sem("ones_in_stacks")
        feat_loaded = [sem(f"features{g}_in_stacks") for g in range(G)]
        kq_made = sem("ffn_weights_quantised")
        x_loaded = sem("x_loaded")
        bn_done = sem("bn_stats_done")
        mv_done = sem("mean_var_done")
        ve_done = sem("var_eps_done")
        rstd_done = sem("rstd_done")
        xn_ready = sem("xn_ready")
        t_ready = sem("xnT_in_psum")
        xb_ready = sem("xnT_bf16_written")
        xh_ready = sem("xnT_hi_written")
        xl_ready = sem("xnT_lo_written")
        qk_ready = sem("qk_in_psum")
        qh_ready = sem("qk_hi_written")
        ql_ready = sem("qk_lo_written")
        qh_copied = sem("qk_hi_copied")
        ql_copied = sem("qk_lo_copied")
        stack_loaded = [sem(f"stack{g}_loaded") for g in range(G)]
        max_loaded = [sem(f"max{g}_in_stack") for g in range(G)]
        s_ready = sem("scores_in_psum")
        max_done = sem("chunk_max_done")
        mh_done = sem("max_hi_done")
        mp_ready = sem("max_parts_ready")
        mt_ready = sem("max_T_in_psum")
        mts_ready = sem("max_T_written")
        st_ready = sem("scoresT_in_psum")
        exp_done = sem("exp_done")
        mask_done = sem("probs_masked")
        pv_done = sem("pv_done")
        ot_ready = sem("out_T_written")
        ot_stored = [sem(f"out_T{i}_regrouped") for i in range(2)]
        den_loaded = [sem(f"denominators{i}_regrouped") for i in range(2)]
        rc_ready = sem("denominators_inverted")
        rc_stored = sem("inverses_stored")
        rb_loaded = sem("inverses_spread")
        div_done = sem("attn_divided")
        ah_ready = sem("attn_hi_written")
        al_ready = sem("attn_lo_written")
        v_ready = sem("v_in_psum")
        va_ready = sem("v_written")
        qt_done = sem("quant_t_done")
        qz_done = sem("quant_over_done")
        qk_magic = sem("quant_guard_done")
        qe_done = sem("quant_exponent_done")
        qm_done = sem("quant_magic_done")
        qr_done = sem("quant_rounded")
        xq_ready = sem("xq_ready")
        ff_ready = sem("ffn_in_psum")
        y1_ready = sem("y1_written")
        y2_ready = sem("y2_written")
        xp_ready = sem("x_plus_bias")
        xy_ready = sem("x_plus_ffn")
        pj_ready = sem("proj_in_psum")
        out_ready = sem("out_written")
        out_stored = sem("out_stored")
        def qk_part(m, part, copy):
            pair = 2 * part + copy if m % 2 == 0 else part + 2 * copy
            return QKP[:, m // 2, pair, m % 2, :]

        def wait_alone(eng, always, *pairs):
            held = [(s, v if isinstance(v, int) else eng.compute_val(v)) for s, v in pairs]
            eng.wait_ge(*always)
            for s, v in held:
                eng.wait_ge(s, v)

        recips = nc.dram_tensor("recips", (H, T), F32, kind="Internal").ap()

        def attn_row(b):
            return AS[:, bass.ds(b % 2, 1), :, :].rearrange("p o a n -> p (o a) n")

        def x_slot(b):
            return X[:, bass.ds(b % 4, 1), :, :].rearrange("p o t c -> p (o t) c")

        block = ctx.enter_context(nc.Block())

        @block.sync
        def _(sp):
            def load_x(b):
                sp.dma_start(x_slot(b), x[bass.ds(b, 1), :, :].rearrange("o (t p) c -> p (o t) c", p=P)) \
                    .then_inc(x_loaded, 16)

            def load_stack(b, g):
                for h in range(HU):
                    r = 64 * (g % 2) + HD * h
                    for a in range(2):
                        sp.dma_start(STK[0:64, g, a, h, :].bitcast(F32),
                                     QKP[r:r + HD, g // 2, :, a, :].bitcast(F32)).then_inc(stack_loaded[g], 16)

            def load_max(b, g):
                sp.wait_ge(mts_ready, 4 * b + g + 1)
                sp.dma_start(STK[K_SCORE:K_ALL, g, 0, :, :].rearrange("p h n -> p (h n)").bitcast(F32),
                             MTS[:, g % 2, :].bitcast(F32)).then_inc(max_loaded[g], 16)

            def regroup(b, g, early):
                if g == 0 and not early:
                    wait_alone(sp, (w_loaded, 16), (al_ready, b), (rc_ready, b), (ot_ready, 4 * b + g + 1))
                else:
                    sp.wait_ge(ot_ready, 4 * b + g + 1)
                for i in range(HU):
                    r = 64 * (g % 2) + HD * i
                    sp.dma_start(attn_row(b)[r:r + HD, g // 2, :],
                                 OT[32 * i:32 * i + HD, g % 2, :]).then_inc(ot_stored[g % 2], 16)
                sp.dma_start(DEN[32 * g:32 * g + 32, :], OT[HD:P:32, g % 2, :]).then_inc(den_loaded[g % 2], 16)

            def store_recips(b):
                wait_alone(sp, (w_loaded, 16), (rc_ready, b + 1), (rb_loaded, 32 * (b + 1)))
                sp.dma_start(recips.rearrange("h (e j) -> (h e) j", e=8), RDEN[:, :]).then_inc(rc_stored, 16)

            def spread_recips(b, last):
                if not last:
                    wait_alone(sp, (w_loaded, 16), (rc_stored, 16 * (b + 1)), (t_ready, 2 * (b + 3)))
                else:
                    sp.wait_ge(rc_stored, 16 * (b + 1))
                    sp.wait_ge(qm_done, B)
                    sp.wait_ge(div_done, b)
                for ct in range(CT):
                    src = recips[8 * ct:8 * ct + 8, :].unsqueeze(1).broadcast_to([8, HD, T])
                    sp.dma_start(RB[:, ct, :], src).then_inc(rb_loaded, 16)

            sp.sem_inc(out_stored, 16)
            sp.sem_inc(rb_loaded, 32)
            load_x(0)
            sp.dma_start(w_raw, w_qkv.rearrange("(m p) c -> p m c", p=P)).then_inc(w_loaded, 16)
            sp.dma_start(BQ[:, :], b_qkv[0:2 * C].rearrange("(m p) -> p m", p=P),
                         allow_slow_non_contiguous=True).then_inc(small_loaded, 16)
            sp.dma_start(SC[:, 0:1], s_in.partition_broadcast(P)).then_inc(small_loaded, 16)
            sp.dma_start(SC[:, 1:2], s_k.partition_broadcast(P)).then_inc(small_loaded, 16)
            sp.dma_start(BV[:, :], b_qkv[2 * C:3 * C].partition_broadcast(P)).then_inc(small_loaded, 16)
            sp.dma_start(BP[:, :], b_proj.partition_broadcast(P)).then_inc(small_loaded, 16)
            sp.dma_start(BF[:, :], ffn_b.partition_broadcast(P)).then_inc(small_loaded, 16)
            sp.dma_start(wp_raw, w_proj.rearrange("(m p) c -> p m c", p=P)).then_inc(small_loaded, 16)
            sp.dma_start(kern_raw, ffn_w.rearrange("(m p) c -> p m c", p=P)).then_inc(small_loaded, 16)
            sp.wait_ge(x_loaded, 16)
            load_x(1)

            def load_features(g):
                for h in range(HU * g, HU * g + HU):
                    r = 16 * (h % 8)
                    if g < 2:
                        sp.dma_start(STK[64:K_SCORE, g, 0, h % HU, :].bitcast(F32),
                                     fq_parts[r:r + 16, :, :].bitcast(F32)).then_inc(feat_loaded[g], 16)
                    sp.dma_start(STK[64:K_SCORE, g, 1, h % HU, :].bitcast(F32),
                                 fk_parts[h // 8][r:r + 16, :, :].bitcast(F32)).then_inc(feat_loaded[g], 16)

            sp.wait_ge(ones_made, 1)
            sp.wait_ge(feat_parts, 2)
            load_features(0)
            load_features(1)
            sp.wait_ge(qh_copied, 2)
            sp.wait_ge(ql_copied, 2)
            load_stack(0, 0)
            load_stack(0, 1)
            sp.wait_ge(feat_parts, 4)
            sp.wait_ge(consts_made, 7)
            load_features(2)
            load_max(0, 0)
            sp.wait_ge(qh_copied, 4)
            sp.wait_ge(ql_copied, 4)
            load_stack(0, 2)
            load_features(3)

            def body(b, first, last, load):
                if load:
                    if not first:
                        sp.wait_ge(out_stored, 16 * b)
                    else:
                        for g in (2, 3):
                            sp.wait_ge(feat_loaded[g], 16 * HU)
                    sp.wait_ge(x_loaded, 16 * (b + 2))
                    load_x(b + 2)
                if not first:
                    sp.wait_ge(st_ready, 44 * b)
                load_stack(b, 3)
                load_max(b, 1)
                if not first:
                    regroup(b - 1, 3, False)
                load_max(b, 2)
                regroup(b, 0, first)
                if not last:
                    wait_alone(sp, (w_loaded, 16), (st_ready, 44 * b + 11),
                               (qh_copied, 4 * (b + 1) + 2), (ql_copied, 4 * (b + 1) + 2))
                    load_stack(b + 1, 0)
                if not first:
                    store_recips(b - 1)
                    spread_recips(b - 1, last)
                if not last:
                    sp.wait_ge(st_ready, 44 * b + 22)
                    load_stack(b + 1, 1)
                load_max(b, 3)
                regroup(b, 1, first)
                if not last:
                    wait_alone(sp, (w_loaded, 16), (st_ready, 44 * b + 33),
                               (qh_copied, 4 * (b + 1) + 4), (ql_copied, 4 * (b + 1) + 4))
                    load_stack(b + 1, 2)
                    load_max(b + 1, 0)
                regroup(b, 2, first)
                if not first:
                    sp.wait_ge(out_ready, 2 * (b + 1))
                    sp.dma_start(out[bass.ds(b - 1, 1), :, :].rearrange("o (t p) c -> p (o t) c", p=P),
                                 x_slot(b + 3)).then_inc(out_stored, 16)

            body(0, True, False, True)
            with sp.Fori(1, B - 2) as b:
                body(b, False, False, True)
            body(B - 2, False, False, False)
            body(B - 1, False, True, False)
            regroup(B - 1, 3, False)
            store_recips(B - 1)
            spread_recips(B - 1, True)
            sp.wait_ge(out_ready, 2 * (B + 1))
            sp.dma_start(out[B - 1:B, :, :].rearrange("o (t p) c -> p (o t) c", p=P), x_slot(B - 1)) \
                .then_inc(out_stored, 16)
            sp.wait_ge(out_stored, 16 * (B + 1))

        @block.tensor
        def _(pe):
            mm = nc.tensor.matmul
            bank_read = [None]

            def misc(*after):
                for read, value in bank_read[0] or ():
                    pe.wait_ge(read, value)
                bank_read[0] = after

            def split3(o, a, b_, n):
                (ah, al), (bh, bl) = a, b_
                for ct in range(CT):
                    for i, (l, r) in enumerate(((ah, bh), (ah, bl), (al, bh))):
                        last = mm(o, l(ct), r(ct), start=(ct == 0 and i == 0), stop=(ct == CT - 1 and i == 2))
                return last

            def job_T(b, ct):
                if ct == 0:
                    pe.wait_ge(xn_ready, b + 1)
                misc((xl_ready, 2 * b + ct + 1))
                for t in range(TT):
                    last = nc.tensor.transpose(MB[:, P * t:P * t + P], XN[:, t, P * ct:P * ct + P], IDF[:, :])
                last.then_inc(t_ready, 1)

            def job_QK(b, m):
                col = P * [0, 2, 1, 3][m]
                if m == 0:
                    pe.wait_ge(xl_ready, 2 * (b + 1))
                misc((ql_ready, 4 * b + m + 1))
                split3(MB[:, :], (lambda ct: WH[:, ct, col:col + P], lambda ct: WL[:, ct, col:col + P]),
                       (lambda ct: XH[:, ct, :], lambda ct: XL[:, ct, :]), T).then_inc(qk_ready, 1)

            def by_tokens(i, ah, al, bh, bl):
                for t in (2 * i, 2 * i + 1):
                    o = MB[:, C * (t % 2):C * (t % 2) + C]
                    last = split3(o, (lambda ct: ah[:, ct, P * t:P * t + P], lambda ct: al[:, ct, P * t:P * t + P]),
                                  (bh, bl), C)
                return last

            def job_V(b, i):
                misc((va_ready, 2 * b + i + 1))
                by_tokens(i, XH, XL, lambda ct: WH[:, ct, 2 * C:3 * C], lambda ct: WL[:, ct, 2 * C:3 * C]) \
                    .then_inc(v_ready, 1)

            def job_PJ(b, i):
                if i == 0:
                    pe.wait_ge(al_ready, b + 2)
                misc((out_ready, 2 * b + i + 3))
                by_tokens(i, AH, AL, lambda ct: PH[:, ct, :], lambda ct: PL[:, ct, :]).then_inc(pj_ready, 1)

            def job_FF(b, i):
                if i == 0:
                    pe.wait_ge(xq_ready, b + 1)
                    pe.wait_ge(kq_made, 1)
                misc((y1_ready, 2 * b + i + 1))
                for t in (2 * i, 2 * i + 1):
                    for ct in range(CT):
                        last = mm(MB[:, C * (t % 2):C * (t % 2) + C], XQ[:, ct, P * t:P * t + P], KQ[:, ct, :],
                                  start=(ct == 0), stop=(ct == CT - 1))
                last.then_inc(ff_ready, 1)

            def job_MT(b, g):
                pe.wait_ge(mp_ready, 4 * b + g + 1)
                misc((mts_ready, 4 * b + g + 1))
                nc.tensor.transpose(MB[0:2 * HU * TT, 0:P], MP[:, g % 2, :, :].rearrange("p a b -> p (a b)"),
                                    IDF[:, :]).then_inc(mt_ready, 1)

            def scores(b, g, c, early=False):
                qt, h0, nh, per = CHUNK_PLAN[c]
                w = P * (qt + 1)
                if c == 0:
                    if isinstance(b, int) and b == 0:
                        pe.wait_ge(feat_loaded[g], 16 * (2 * HU if g < 2 else HU))
                    pe.wait_ge(stack_loaded[g], 128 * (b + 1))
                if not (early and g == 0 and c < 2):
                    pe.wait_ge(max_done, 24 * b + 6 * g + c - 1)
                buf = SB_[c % 2]
                for i in range(nh):
                    h, o = h0 + i, w * (i % per)
                    mm(buf[:, i // per, o:o + w], STK[0:K_SCORE, g, 0, h, P * qt:P * qt + P],
                       STK[0:K_SCORE, g, 1, h, 0:w], start=True, stop=False)
                    last = mm(buf[:, i // per, o + w - P:o + w], CMT[:, :], IDB[:, :], start=False, stop=True)
                last.then_inc(s_ready, 1)

            def scores_T(b, g, k, first):
                j, h0, nh = SLOT_PLAN[k]
                w = WJ[j]
                if k == 0:
                    pe.wait_ge(max_loaded[g], 16 * (b + 1))
                if not (first and g == 0 and k < 2):
                    pe.wait_ge(exp_done, 44 * b + 11 * g + k - 1)
                bank = STB[(11 * g + k) % 2]
                for i in range(nh):
                    h = h0 + i
                    last = mm(bank[:, w * i:w * i + w], STK[0:K_ALL, g, 1, h, P * j:P * j + P],
                              STK[0:K_ALL, g, 0, h, P * j:T], start=True, stop=True)
                last.then_inc(st_ready, 1)

            def pv(b, g, j, first):
                pe.wait_ge(mask_done, 16 * b + 4 * g + j + 1)
                if j == 0:
                    if g == 0:
                        pe.wait_ge(va_ready, 2 * (b + 1))
                    if not (first and g == 0):
                        pe.wait_ge(ot_ready, 4 * b + g)
                for i in range(HU):
                    last = mm(PVB[32 * i:32 * i + 32, P * j:T],
                              VA[:, j, HU * g + i, :, :].rearrange("p a d -> p (a d)"),
                              PJ[j][:, i, :], start=(j == 0), stop=(j == TT - 1))
                last.then_inc(pv_done, 1)

            pe.sem_inc(pj_ready, 2)
            pe.wait_ge(ident_steps, 3)
            pe.wait_ge(w_loaded, 16)
            for n in range(4):
                ct, half = n // 2, n % 2
                for m in range(3):
                    last = nc.tensor.transpose(SB_[n // 2][:, n % 2, P * m:P * m + P],
                                               w_raw[:, 3 * half + m, P * ct:P * ct + P], IDF[:, :])
                last.then_inc(setup_T, 1)
            pe.wait_ge(small_loaded, 16 * 8)
            for ct in range(CT):
                for m in range(2):
                    last = nc.tensor.transpose(STB[ct][:, P * m:P * m + P], wp_raw[:, m, P * ct:P * ct + P], IDF[:, :])
                last.then_inc(setup_T, 1)
            for ct in range(CT):
                job_T(0, ct)
            pe.wait_ge(setup_lo, 6)
            for m in range(4):
                job_QK(0, m)
            pe.wait_ge(consts_made, 8)
            for c in range(CHUNKS):
                scores(0, 0, c, True)
            job_MT(0, 0)
            for c in range(CHUNKS):
                scores(0, 1, c, True)

            def body(b, first, last):
                if not first:
                    bank_read[0] = last_job(b)
                for g in range(G):
                    nb, ng = (b, g + 2) if g < 2 else (b + 1, g - 2)
                    ahead = not (last and g >= 2)
                    for k in range(SLOTS):
                        scores_T(b, g, k, first)
                        if k % 2 == 0 and ahead:
                            scores(nb, ng, k // 2)
                        pb, pg = (b, g - 1) if g else (b - 1, 3)
                        if k in PV_AT[2:] and not (first and g == 0):
                            pv(pb, pg, PV_AT.index(k), False)
                        if (g, k) in V_AT:
                            job_V(b, V_AT.index((g, k)))
                        if k == MT_AT[g] and not (last and g == 3):
                            job_MT(*((b, g + 1) if g < 3 else (b + 1, 0)))
                        if (g, k) in T_AT and not last:
                            job_T(b + 1, T_AT.index((g, k)))
                        if (g, k) in QK_AT and not last:
                            job_QK(b + 1, QK_AT.index((g, k)))
                        if (g, k) in FF_AT:
                            job_FF(b, FF_AT.index((g, k)))
                        if (g, k) in PJ_AT and not first:
                            job_PJ(b - 1, PJ_AT.index((g, k)))
                        if k in PV_AT[:2]:
                            pv(b, g, PV_AT.index(k), first)

            body(0, True, False)
            for read, value in bank_read[0]:
                pe.wait_ge(read, value)
            with pe.Fori(1, B - 1) as b:
                last_job = lambda b: ((out_ready, 2 * b),)
                body(b, False, False)
            body(B - 1, False, True)
            for j in (2, 3):
                pv(B - 1, 3, j, False)
            for i in range(2):
                job_PJ(B - 1, i)

        @block.scalar
        def _(act):
            A = nc.scalar.activation

            act.dma_start(fq_raw, feat_q).then_inc(feat_raw, 16)
            act.dma_start(fk_raw, feat_k).then_inc(feat_raw, 16)
            act.dma_start(POS[:, :], pos.rearrange("a b -> (a b)").rearrange("(p o) -> p o", o=1)) \
                .then_inc(feat_raw, 16)

            def T_evac(b, ct):
                act.wait_ge(t_ready, 2 * b + ct + 1)
                A(XB[:, ct, :], MB[:, :], ACT.Copy).then_inc(xb_ready, 1)
                A(XH[:, ct, :], MB[:, :], ACT.Copy).then_inc(xh_ready, 1)

            def QK_evac(b, m, first):
                act.wait_ge(qk_ready, 4 * b + m + 1)
                if not first:
                    for g in ((0, 1) if m < 2 else (2, 3)):
                        act.wait_ge(stack_loaded[g], 128 * b)
                bias = [0, 2, 1, 3][m]
                A(qk_part(m, 0, 0), MB[:, :], ACT.Identity, bias=BQ[:, bias:bias + 1]).then_inc(qh_ready, 1)
                act.wait_ge(qh_ready, 4 * b + m + 1)
                A(qk_part(m, 0, 1), qk_part(m, 0, 0).bitcast(F32), ACT.Copy).then_inc(qh_copied, 1)

            for n in range(4):
                ct, half = n // 2, n % 2
                act.wait_ge(setup_T, n + 1)
                src = SB_[n // 2][:, n % 2, 0:3 * P]
                if half == 0:
                    A(WH[:, ct, 0:C], src[:, 0:C], ACT.Copy, scale=HD ** -0.5)
                    A(WH[:, ct, C:3 * P], src[:, C:3 * P], ACT.Copy).then_inc(setup_hi, 1)
                else:
                    A(WH[:, ct, 3 * P:3 * C], src, ACT.Copy).then_inc(setup_hi, 1)
            for ct in range(CT):
                act.wait_ge(setup_T, 5 + ct)
                A(PH[:, ct, :], STB[ct][:, 0:C], ACT.Copy).then_inc(setup_hi, 1)
            for ct in range(CT):
                T_evac(0, ct)
            act.wait_ge(setup_step, 6)
            for m in range(4):
                QK_evac(0, m, True)

            def out_T(b, g, skip_wait):
                act.wait_ge(pv_done, 16 * b + 4 * g + 4)
                if not skip_wait:
                    act.wait_ge(ot_stored[g % 2], 64 * (2 * b + g // 2))
                    act.wait_ge(den_loaded[g % 2], 16 * (2 * b + g // 2))
                A(OT[:, g % 2, :], PVB[:, :], ACT.Copy).then_inc(ot_ready, 1)

            def body(b, first, last):
                for g in range(G):
                    for k in range(SLOTS):
                        j, h0, nh = SLOT_PLAN[k]
                        act.wait_ge(st_ready, 44 * b + 11 * g + k + 1)
                        if k in (0, 4, 8, 10) and not (first and g == 0):
                            act.wait_ge(pv_done, 16 * b + 4 * g + j - 3)
                        A(PJ[j][:, h0:h0 + nh, :], STB[(11 * g + k) % 2][:, 0:nh * WJ[j]]
                          .rearrange("p (h n) -> p h n", h=nh), ACT.Exp).then_inc(exp_done, 1)
                        pb, pg = (b, g - 1) if g else (b - 1, 3)
                        if not (first and g == 0):
                            if k == OUT_AT:
                                out_T(pb, pg, first and pg < 2)
                        if (g, k) in T_AT and not last:
                            i = T_AT.index((g, k))
                            if i == 0 and not first:
                                act.wait_ge(xy_ready, b)
                            T_evac(b + 1, i)
                        if (g, k) in QK_AT and not last:
                            QK_evac(b + 1, QK_AT.index((g, k)), False)
                        if (g, k) in FF_AT:
                            i = FF_AT.index((g, k))
                            act.wait_ge(ff_ready, 2 * b + i + 1)
                            if i == 0 and not last:
                                act.wait_ge(qz_done, b + 2)
                            A(Y1[:, 2 * i:2 * i + 2, :], MB[:, :].rearrange("p (t c) -> p t c", c=C),
                              ACT.Identity, scale=SC[:, 3:4]).then_inc(y1_ready, 1)

            body(0, True, False)
            with act.Fori(1, B - 1) as b:
                body(b, False, False)
            body(B - 1, False, True)
            out_T(B - 1, 3, False)

        @block.vector
        def _(dve):
            V = nc.vector

            def stats(b):
                dve.wait_ge(x_loaded, 16 * (b + 1))
                for t in range(TT):
                    V.bn_stats(ST6[:, t, :], x_slot(b)[:, t, :]).then_inc(bn_done, 1)
                for t in range(TT):
                    wait_alone(dve, (x_loaded, 16), (bn_done, 4 * b + t + 1))
                    V.bn_aggr(MV[:, t, :], ST6[:, t, :]).then_inc(mv_done, 1)
                dve.wait_ge(mv_done, 4 * b + 4)
                V.tensor_scalar(VE[:, :], MV[:, :, 1], EPS, None, ALU.add).then_inc(ve_done, 1)

            def normalise(b):
                dve.wait_ge(rstd_done, b + 1)
                dve.wait_ge(t_ready, 2 * b)
                dve.wait_ge(qm_done, b)
                for t in range(TT):
                    ins = V.tensor_scalar(XN[:, t, :], x_slot(b)[:, t, :], MV[:, t, 0:1], RSTD[:, t:t + 1],
                                          ALU.subtract, ALU.mult)
                ins.then_inc(xn_ready, 1)

            def T_lo(b, ct):
                dve.wait_ge(xh_ready, 2 * b + ct + 1)
                V.tensor_tensor(XL[:, ct, :], MB[:, :], XH[:, ct, :].bitcast(F32), ALU.subtract) \
                    .then_inc(xl_ready, 1)

            def QK_lo(b, m):
                bias = [0, 2, 1, 3][m]
                dve.wait_ge(qh_ready, 4 * b + m + 1)
                V.scalar_tensor_tensor(out=qk_part(m, 1, 0), in0=MB[:, :], scalar=BQ[:, bias:bias + 1],
                                       in1=qk_part(m, 0, 0).bitcast(F32), op0=ALU.add, op1=ALU.subtract) \
                    .then_inc(ql_ready, 1)
                dve.wait_ge(ql_ready, 4 * b + m + 1)
                V.tensor_copy(qk_part(m, 1, 1), qk_part(m, 1, 0).bitcast(F32)).then_inc(ql_copied, 1)

            def chunk_max(b, g, c):
                qt, h0, nh, per = CHUNK_PLAN[c]
                w = P * (qt + 1)
                buf = SB_[c % 2]
                src = (buf[:, :, 0:w] if per == 1 else buf[:, :, :].rearrange("p b (h w) -> p (b h) w", w=w)
                       if per == 2 else buf[:, 0, :].rearrange("p (h w) -> p h w", w=w))
                dve.wait_ge(s_ready, 24 * b + 6 * g + c + 1)
                V.tensor_reduce(MX[:, g % 2, h0:h0 + nh, qt], src, AX_X, ALU.max, negate=True) \
                    .then_inc(max_done, 1)

            def max_parts(b, g):
                p = g % 2
                mx = MX[:, p, :, :].rearrange("p h t -> p (h t)")
                dve.wait_ge(max_done, 24 * b + 6 * g + 6)
                V.tensor_copy(MP[:, p, 0, :].bitcast(F32R), mx).then_inc(mh_done, 1)
                dve.wait_ge(mh_done, 4 * b + g + 1)
                V.tensor_tensor(MP[:, p, 1, :], mx, MP[:, p, 0, :], ALU.subtract).then_inc(mp_ready, 1)

            def max_T(b, g):
                dve.wait_ge(mt_ready, 4 * b + g + 1)
                V.tensor_copy(MTS[:, g % 2, :], MB[0:2 * HU * TT, 0:P]).then_inc(mts_ready, 1)

            def v_evac(b, i, first):
                dve.wait_ge(v_ready, 2 * b + i + 1)
                if i == 0 and not first:
                    dve.wait_ge(pv_done, 16 * b)
                V.tensor_tensor(VA[:, 2 * i:2 * i + 2, :, 0, :],
                                MB[:, :].rearrange("p (t h d) -> p t h d", h=H, d=HD),
                                BV[:, :].rearrange("p (h d) -> p h d", d=HD).unsqueeze(1).broadcast_to([P, 2, H, HD]),
                                ALU.add).then_inc(va_ready, 1)

            def invert(b):
                for i in range(2):
                    dve.wait_ge(den_loaded[i], 32 * (b + 1))
                V.reciprocal(RDEN[:, :], DEN[:, :]).then_inc(rc_ready, 1)

            def divide(b):
                dve.wait_ge(rb_loaded, 32 * (b + 2))
                for i in range(2):
                    dve.wait_ge(ot_stored[i], 128 * (b + 1))
                V.tensor_tensor(attn_row(b), attn_row(b), RB, ALU.mult).then_inc(div_done, 1)
                wait_alone(dve, (x_loaded, 16), (pj_ready, 2 * (b + 1)), (div_done, b + 1))
                V.tensor_scalar(AH[:, :, :], attn_row(b), 1.0, None, ALU.mult).then_inc(ah_ready, 1)

            def result(b, i):
                dve.wait_ge(pj_ready, 2 * b + i + 3)
                dve.wait_ge(xy_ready, b + 1)
                xs = x_slot(b + 4)[:, 2 * i:2 * i + 2, :]
                V.tensor_tensor(xs, MB[:, :].rearrange("p (t c) -> p t c", c=C), xs, ALU.add) \
                    .then_inc(out_ready, 1)

            def quant_magic(b):
                if isinstance(b, int) and b < 2:
                    dve.wait_ge(qk_magic, b + 1)
                else:
                    wait_alone(dve, (x_loaded, 16), (qk_magic, b + 1), (div_done, b - 1))
                V.tensor_scalar(QE.bitcast(I32), QT.bitcast(I32), 0x7F800000, None, ALU.bitwise_and) \
                    .then_inc(qe_done, 1)
                dve.wait_ge(qe_done, b + 1)
                V.scalar_tensor_tensor(out=QM, in0=QE, scalar=E4_LEAST, in1=QM, op0=ALU.max, op1=ALU.mult) \
                    .then_inc(qm_done, 1)

            step = [0]

            def then(ins):
                step[0] += 1
                ins.then_inc(setup_step, 1)
                dve.wait_ge(setup_step, step[0])

            dve.sem_inc(out_ready, 2)
            V.memset(STK[96:P, 0:2, 1, :, :].bitcast(F32), 1.0).then_inc(ones_made, 1)
            stats(0)
            dve.wait_ge(feat_raw, 48)
            for raw, parts, order in ((fq_raw, fq_parts, (0, 1, 2)), (fk_raw, fk_parts[0], (0, 2, 1))):
                V.tensor_copy(parts[:, order[1], :], raw)
                then(V.tensor_copy(parts[:, order[0], :], raw))
                V.tensor_tensor(parts[:, order[2], :], raw, parts[:, order[0], :].bitcast(F32), ALU.subtract) \
                    .then_inc(feat_parts, 1)
            dve.wait_ge(rstd_done, 1)
            for t in range(TT):
                ins = V.tensor_scalar(XN[:, t, :], x_slot(0)[:, t, :], MV[:, t, 0:1], RSTD[:, t:t + 1],
                                      ALU.subtract, ALU.mult)
            ins.then_inc(xn_ready, 1)
            dve.wait_ge(small_loaded, 16 * 8)
            then(V.tensor_scalar(BQ[:, 0:2], BQ[:, 0:2], HD ** -0.5, None, ALU.mult))
            then(V.reciprocal(SC[:, 4:5], SC[:, 1:2]))
            then(V.reciprocal(SC[:, 2:3], SC[:, 0:1]))
            then(V.tensor_tensor(SC[:, 3:4], SC[:, 0:1], SC[:, 1:2], ALU.mult))
            for n in range(4):
                ct, half = n // 2, n % 2
                src = SB_[n // 2][:, n % 2, 0:3 * P]
                dve.wait_ge(setup_hi, n + 1)
                if half == 0:
                    V.scalar_tensor_tensor(out=WL[:, ct, 0:C], in0=src[:, 0:C], scalar=HD ** -0.5,
                                           in1=WH[:, ct, 0:C].bitcast(F32), op0=ALU.mult, op1=ALU.subtract)
                    V.tensor_tensor(WL[:, ct, C:3 * P], src[:, C:3 * P], WH[:, ct, C:3 * P].bitcast(F32),
                                    ALU.subtract).then_inc(setup_lo, 1)
                else:
                    V.tensor_tensor(WL[:, ct, 3 * P:3 * C], src, WH[:, ct, 3 * P:3 * C].bitcast(F32),
                                    ALU.subtract).then_inc(setup_lo, 1)
            for ct in range(CT):
                dve.wait_ge(setup_hi, 5 + ct)
                V.tensor_tensor(PL[:, ct, :], STB[ct][:, 0:C], PH[:, ct, :].bitcast(F32), ALU.subtract) \
                    .then_inc(setup_lo, 1)
            for ct in range(CT):
                T_lo(0, ct)
            for m in (0, 1):
                QK_lo(0, m)
            pos_rows = POS[:, 0:1].broadcast_to([P, T])
            V.memset(fk_parts[1][:, 2, :].bitcast(F32), 0.0).then_inc(feat_parts, 1)
            then(V.tensor_copy(fk_parts[1][:, 0, :], pos_rows))
            V.tensor_tensor(fk_parts[1][:, 1, :], pos_rows, fk_parts[1][:, 0, :].bitcast(F32), ALU.subtract) \
                .then_inc(feat_parts, 1)
            for m in (2, 3):
                QK_lo(0, m)
            for c in range(CHUNKS):
                chunk_max(0, 0, c)
            max_parts(0, 0)
            max_T(0, 0)
            kt, ke, km = QZ[:, 0, 0, :], QZ[:, 0, 1, :], QZ[:, 1, 0, :]
            kr = XQ[:, 0, :]
            then(V.tensor_scalar(kt, kr, SC[:, 4:5], None, ALU.mult))
            then(V.tensor_scalar(km, kt, E4_OVER, None, ALU.mult))
            then(V.tensor_scalar(km, km, 0.0, E4_MAGIC, ALU.mult, ALU.add))
            then(V.tensor_scalar(ke.bitcast(I32), kt.bitcast(I32), 0x7F800000, None, ALU.bitwise_and))
            then(V.scalar_tensor_tensor(out=km, in0=ke, scalar=E4_LEAST, in1=km, op0=ALU.max, op1=ALU.mult))
            then(V.tensor_tensor(kt, kt, km, ALU.add))
            V.tensor_tensor(KQ[:, :, :].rearrange("p a c -> p (a c)"), kt, km, ALU.subtract).then_inc(kq_made, 1)
            stats(1)
            for c in range(CHUNKS):
                chunk_max(0, 1, c)
            max_parts(0, 1)
            quant_magic(0)
            normalise(1)

            def body(b, first, last, more):
                for g in range(G):
                    nb, ng = (b, g + 2) if g < 2 else (b + 1, g - 2)
                    ahead = not (last and g >= 2)
                    for k in range(SLOTS):
                        if k % 2 == 0 and ahead:
                            chunk_max(nb, ng, k // 2)
                        if (g, k) in V_AT:
                            v_evac(b, V_AT.index((g, k)), first)
                        if k == MT_AT[g] and not (last and g == 3):
                            max_T(*((b, g + 1) if g < 3 else (b + 1, 0)))
                        if (g, k) in T_AT and not last:
                            T_lo(b + 1, T_AT.index((g, k)))
                        if (g, k) in QK_AT and not last:
                            QK_lo(b + 1, QK_AT.index((g, k)))
                        if (g, k) in PJ_AT and not first:
                            result(b - 1, PJ_AT.index((g, k)))
                        if (g, k) == INVERT_AT and not first:
                            invert(b - 1)
                        if (g, k) == DIVIDE_AT and not first:
                            divide(b - 1)
                        if (g, k) == STATS_AT and more:
                            stats(b + 2)
                        if (g, k) == MAGIC_AT and not last:
                            quant_magic(b + 1)
                        if (g, k) == NORM_AT and more:
                            normalise(b + 2)
                    if ahead:
                        max_parts(nb, ng)

            body(0, True, False, True)
            with dve.Fori(1, B - 2) as b:
                body(b, False, False, True)
            body(B - 2, False, False, False)
            body(B - 1, False, True, False)
            invert(B - 1)
            divide(B - 1)
            for i in range(2):
                result(B - 1, i)

        @block.gpsimd
        def _(pool):
            GP = nc.gpsimd

            def rstd(b):
                pool.wait_ge(ve_done, b + 1)
                GP.tensor_tensor(RSTD[:, :], VE[:, :], NH[:, :], ALU.pow).then_inc(rstd_done, 1)

            def quant_scale(b):
                wait_alone(pool, (ident_steps, 3), (xb_ready, 2 * (b + 1)))
                GP.tensor_scalar(QT, XB[:, :, :], SC[:, 2:3], 1.0, ALU.mult, ALU.mult).then_inc(qt_done, 1)
                GP.tensor_scalar(QM, XB[:, :, :], SC[:, 2:3], E4_OVER, ALU.mult, ALU.mult).then_inc(qz_done, 1)
                wait_alone(pool, (ident_steps, 3), (qz_done, b + 1))
                GP.tensor_scalar(QM, QM, 0.0, E4_MAGIC, ALU.mult, ALU.add).then_inc(qk_magic, 1)

            def quant_round(b):
                pool.wait_ge(qm_done, b + 1)
                GP.tensor_tensor(QT, QT, QM, ALU.add).then_inc(qr_done, 1)

            def quant_write(b):
                pool.wait_ge(qr_done, b + 1)
                pool.wait_ge(ff_ready, 2 * b)
                GP.tensor_tensor(XQ[:, :, :], QT, QM, ALU.subtract).then_inc(xq_ready, 1)

            def mask(b, g, j):
                wait_alone(pool, (ident_steps, 3), (exp_done, 44 * b + 11 * g + LAST_SLOT[j] + 1))
                d = PJ[j][:, :, 0:P]
                GP.affine_select(out=d, in_=d, compare_op=ALU.is_ge, fill=0.0, base=0,
                                 pattern=[[0, HU], [1, P]], channel_multiplier=-1).then_inc(mask_done, 1)

            def ffn_bias(b):
                pool.wait_ge(y1_ready, 2 * (b + 1))
                GP.tensor_tensor(Y1[:, :, :], Y1[:, :, :], BF[:, :].unsqueeze(1).broadcast_to([P, TT, C]),
                                 ALU.add).then_inc(y2_ready, 1)

            def add_ffn(b):
                pool.wait_ge(y2_ready, b + 1)
                pool.wait_ge(xp_ready, b + 1)
                xs = x_slot(b + 4)
                GP.tensor_tensor(xs, xs, Y1[:, :, :], ALU.add).then_inc(xy_ready, 1)

            def add_bias(b):
                pool.wait_ge(xn_ready, b + 1)
                xs = x_slot(b)
                GP.tensor_tensor(xs, xs, BP[:, :].unsqueeze(1).broadcast_to([P, TT, C]), ALU.add) \
                    .then_inc(xp_ready, 1)

            def attn_parts(b):
                pool.wait_ge(ah_ready, b + 1)
                GP.tensor_tensor(AL[:, :, :], attn_row(b), AH[:, :, :].bitcast(F32), ALU.subtract) \
                    .then_inc(al_ready, 1)

            pool.sem_inc(al_ready, 1)
            GP.memset(IDF[:, :], 0.0).then_inc(ident_steps, 1)
            pool.wait_ge(ident_steps, 1)
            GP.affine_select(out=IDF[:, :], in_=IDF[:, :], compare_op=ALU.not_equal, fill=1.0, base=0,
                             pattern=[[-1, P]], channel_multiplier=1).then_inc(ident_steps, 2)
            GP.memset(IDB[:, :], 0.0).then_inc(consts_made, 1)
            GP.memset(CMT[:, :], 0.0).then_inc(consts_made, 1)
            pool.wait_ge(consts_made, 2)
            GP.affine_select(out=IDB[:, :], in_=IDB[:, :], compare_op=ALU.not_equal, fill=1.0, base=0,
                             pattern=[[-1, P]], channel_multiplier=1).then_inc(consts_made, 1)
            GP.affine_select(out=CMT[:, :], in_=CMT[:, :], compare_op=ALU.is_ge, fill=MASKED, base=0,
                             pattern=[[1, P]], channel_multiplier=-1).then_inc(consts_made, 1)
            GP.memset(NH[:, :], -0.5).then_inc(consts_made, 1)
            pool.wait_ge(consts_made, 5)
            GP.memset(STK[96:P, 2:4, 1, :, :].bitcast(F32), 1.0).then_inc(consts_made, 1)
            pool.wait_ge(consts_made, 6)
            rstd(0)
            pool.wait_ge(rstd_done, 1)
            GP.memset(STK[64:P, 2:4, 0, :, :].bitcast(F32), 1.0).then_inc(consts_made, 1)
            pool.wait_ge(consts_made, 7)
            GP.memset(VA[:, :, :, 1, :].rearrange("p t h d -> p (t h) d"), 1.0).then_inc(consts_made, 1)
            pool.wait_ge(kq_made, 1)
            quant_scale(0)
            rstd(1)
            quant_round(0)
            quant_write(0)

            def body(b, first, last, more):
                for g in range(G):
                    if g == 0 and not first:
                        ffn_bias(b - 1)
                        add_ffn(b - 1)
                    if g == 1 and not last:
                        quant_scale(b + 1)
                    if g == 3 and not last:
                        quant_round(b + 1)
                    if g == 3 and more:
                        rstd(b + 2)
                    mask(b, g, 0)
                    if g == 1:
                        add_bias(b)
                    if g == 2 and not first:
                        attn_parts(b - 1)
                    if g == 3 and not last:
                        quant_write(b + 1)
                    for j in (1, 2, 3):
                        mask(b, g, j)

            body(0, True, False, True)
            with pool.Fori(1, B - 2) as b:
                body(b, False, False, True)
            body(B - 2, False, False, False)
            body(B - 1, False, True, False)
            ffn_bias(B - 1)
            add_ffn(B - 1)
            attn_parts(B - 1)

    return nc


_INS = ["L0_attn_x", "L0_attn_w_qkv", "L0_attn_b_qkv", "L0_attn_w_proj", "L0_attn_b_proj",
        "L0_attn_pos_independent", "L0_ffn_kernel", "L0_ffn_input_scale", "L0_ffn_kernel_scale", "L0_ffn_bias"]


def kernel(**inputs):
    import numpy as _np
    import concourse.bacc as _bacc
    from concourse import mybir as _mybir
    from concourse.bass_utils import run_bass_kernel_spmd as _run

    nc = _bacc.Bacc("TRN2", target_bir_lowering=False, num_devices=1)
    arrays, args = {}, []

    def give(name, a):
        arrays[name] = a
        args.append(nc.dram_tensor(name, a.shape, _mybir.dt.from_np(a.dtype), kind="ExternalInput").ap())

    for name in _INS:
        give(f"in_{name}", _np.ascontiguousarray(inputs[name]))
    for name, table in zip(("feature_q", "feature_k"), position_tables()):
        give(name, table)
    args.append(nc.dram_tensor("out", (B, T, C), F32, kind="ExternalOutput").ap())
    build(nc, *args)
    r = _run(nc, [arrays], core_ids=[0])
    return r.results[0]["out"]
```

```python
from contextlib import ExitStack

import numpy as np

import concourse.bass as bass
from concourse import mybir

P = 128
B, T, C = 16, 512, 256
H, HD = 16, 16
TT = T // P
CT = C // P
G = 4
HU = H // G
BASE = 2500
EPS = 1e-5
K_SCORE = 112
K_ALL = 114
SLOTS = 11
CHUNKS = 11
ROW = G * SLOTS
WJ = [T - P * j for j in range(TT)]
SLOT_PLAN = [(0, h, 1) for h in range(4)] + [(1, h, 1) for h in range(4)] + [(2, 0, 2), (2, 2, 2), (3, 0, 4)]
LAST_SLOT = [3, 7, 9, 10]
CHUNK_PLAN = [(3, h, 1) for h in range(4)] + [(2, h, 1) for h in range(4)] + [(1, 0, 2), (1, 2, 2), (0, 0, 4)]
V_AT = [(0, 2), (0, 3)]
T_AT = [(0, 6), (0, 10)]
QK_AT = [(1, 2), (1, 3), (1, 6), (1, 9)]
FF_AT = [(2, 6), (2, 7)]
PJ_AT = [(3, 3), (3, 6)]
MT_AT = [(0, 5), (1, 0), (2, 5), (3, 2)]
ACT_LAG = {"T": 0, "QK": 0, "FF": 1, "copy_lo": 1}
DVE_LAG = {"V": 0, "T": 1, "QK": 0, "PJ": 1, "MT": 0, "copy_hi": 0}
PV_AT = [7, 10, 0, 1]
OUT_AT = 1
AH_AT = [(2, 5), (2, 5)]
INVERT_AT, DIVIDE_AT = (1, 0), (2, 4)
STATS_AT, NORM_AT = (2, 6), (3, 9)
MAGIC_AT = (3, 0)
ORDER = [job for _, job in sorted([(at, (kind, i)) for kind, ats in (
    ("V", V_AT), ("T", T_AT), ("QK", QK_AT), ("FF", FF_AT), ("PJ", PJ_AT), ("MT", MT_AT))
    for i, at in enumerate(ats)])]
MISC_BANK = {job: n % 2 for n, job in enumerate(ORDER)}
MASKED = -1.0e30
E4_LEAST = 2.0 ** -6
E4_MAGIC = 1.5 * 2.0 ** 20
E4_OVER = float(np.finfo(np.float32).max / np.float32(464.0))

F32 = mybir.dt.float32
F32R = mybir.dt.float32r
BF16 = mybir.dt.bfloat16
I32 = mybir.dt.int32
ALU = mybir.AluOpType
ACT = mybir.ActivationFunctionType
AX_X = mybir.AxisListType.X


def due(jobs, g, k, lag=0):
    return [i for i, (jg, jk) in enumerate(jobs) if SLOTS * jg + jk == SLOTS * g + k - lag]


def position_tables():
    dim = C // 2
    freqs = (1.0 / BASE ** (np.arange(dim, dtype=np.float64) / dim))[: dim - C // 4].astype(np.float32)
    angle = np.arange(T, dtype=np.float64)[None, :] * freqs.astype(np.float64)[:, None]
    c, s = np.cos(angle).reshape(8, 8, T), np.sin(angle).reshape(8, 8, T)
    q = np.concatenate([c, s], axis=1).reshape(P, T)
    k = np.concatenate([c - s, c + s], axis=1).reshape(P, T)
    return q.astype(np.float32), k.astype(np.float32)


def build(nc, x, w_qkv, b_qkv, w_proj, b_proj, pos, ffn_w, s_in, s_k, ffn_b, feat_q, feat_k, out):
    with ExitStack() as ctx:
        def sb(name, shape, dt):
            return ctx.enter_context(nc.sbuf_tensor(name, shape, dt))

        def ps(name, shape):
            return ctx.enter_context(nc.psum_tensor(name, shape, F32))

        def sem(name):
            return ctx.enter_context(nc.semaphore(name))

        STK = sb("stacks", [P, G, 2, HU, T], F32R)
        PROBS = sb("probs", [P, HU * sum(WJ)], F32)
        PJ = [PROBS[:, HU * sum(WJ[:j]):HU * sum(WJ[:j + 1])].rearrange("p (h n) -> p h n", h=HU) for j in range(TT)]
        X = sb("x_ring", [P, 4, TT, C], F32)
        XN = sb("xn", [P, TT, C], F32)
        XH = sb("xnT_hi", [P, CT, T], F32R)
        XL = sb("xnT_lo", [P, CT, T], F32R)
        QKP = sb("qk_parts", [P, 2, 4, 2, T], F32R)
        VA = sb("v_ones", [P, TT, H, 2, HD], F32)
        OT = sb("out_T", [P, 2, T], F32)
        AS = sb("attn", [P, 2, CT, T], F32)
        DEN = sb("denominators", [P, T // 8], F32)
        RDEN = sb("denominators_inv", [P, T // 8], F32)
        AH = sb("attn_hi", [P, CT, T], F32R)
        AL = sb("attn_lo", [P, CT, T], F32R)
        XB = sb("xnT_bf16", [P, CT, T], BF16)
        QZ = sb("quant_work", [P, 2, CT, T], F32)
        QT, QM = QZ[:, 0], QZ[:, 1]
        QE = XN[:, :, :].rearrange("p t c -> p (t c)").rearrange("p (a n) -> p a n", n=T)
        XQ = sb("xq", [P, CT, T], BF16)
        Y1 = XB[:, :, :].rearrange("p a n -> p (a n)").rearrange("p (t c) -> p t c", c=C)
        MX = sb("neg_max", [P, 2, HU, TT], F32)
        MP = sb("neg_max_parts", [P, 2, 2, HU * TT], F32)
        MTS = sb("neg_max_T", [2 * HU * TT, 2, P], F32R)
        ST6 = sb("bn_six", [P, TT, 6], F32)
        MV = sb("mean_var", [P, TT, 2], F32)
        VE = sb("var_eps", [P, TT], F32)
        RSTD = sb("rstd", [P, TT], F32)
        NH = sb("neg_half", [P, TT], F32)
        WH = sb("w_qkvT_hi", [P, CT, 3 * C], F32R)
        WL = sb("w_qkvT_lo", [P, CT, 3 * C], F32R)
        PH = sb("w_projT_hi", [P, CT, C], F32R)
        PL = sb("w_projT_lo", [P, CT, C], F32R)
        KQ = sb("ffn_w_q", [P, CT, C], BF16)
        IDF = sb("ident_f32", [P, P], F32)
        IDB = sb("ident_bf16", [P, P], BF16)
        CMT = sb("causal_mask_T", [P, P], BF16)
        BQ = sb("b_qk", [P, 4], F32)
        BV = sb("b_v", [P, C], F32)
        BP = sb("b_proj", [P, C], F32)
        BF = sb("b_ffn", [P, C], BF16)
        SC = sb("ffn_scales", [P, 5], F32)
        POS = sb("pos_col", [P, 1], F32)
        RB = QE
        slabs = PROBS[:, :].rearrange("p (s n) -> p s n", n=T)
        w_raw = slabs[:, 0:3, :].rearrange("p s n -> p (s n)").rearrange("p (m c) -> p m c", c=C)
        wp_raw = AS[:, 0, 0, :].rearrange("p (b c) -> p b c", c=C)
        fq_raw, fk_raw = AS[:, 1, 0, :], AS[:, 1, 1, :]
        kt, ke, km = QZ[:, 0, 0, :], QZ[:, 0, 1, :], QZ[:, 1, 0, :]
        kern_raw = XQ[:, 0, :].rearrange("p (a c) -> p a c", c=C)
        x_tail = X[:, 2:4, :, :].rearrange("p s t c -> p (s t c)")[:, 0:3 * T]
        fq_parts = slabs[:, 3:6, :].bitcast(F32R)
        fk_parts = [slabs[:, 6:9, :].bitcast(F32R), x_tail.rearrange("p (r n) -> p r n", n=T).bitcast(F32R)]

        SB_ = [ps(f"score_{i}", [P, 512]) for i in "abc"]
        STB = [ps("scoreT_a", [P, 512]), ps("scoreT_b", [P, 512])]
        PVB = ps("pv", [P, 512])
        MBS = [ps("misc_a", [P, 512]), ps("misc_b", [P, 512])]
        w_banks = SB_ + [PVB]

        w_loaded = sem("weights_loaded")
        small_loaded = sem("small_inputs_loaded")
        consts_made = sem("constants_made")
        ident_steps = sem("identity_steps")
        feat_raw = sem("features_loaded_raw")
        setup_T = sem("setup_transposed")
        setup_hi = sem("setup_hi_written")
        setup_lo = sem("setup_lo_written")
        setup_step = sem("setup_vector_steps")
        feat_parts = sem("feature_parts_made")
        ones_made = sem("ones_in_stacks")
        feat_loaded = [sem(f"features{g}_in_stacks") for g in range(G)]
        kq_step = sem("ffn_weight_steps")
        kq_made = sem("ffn_weights_quantised")
        x_loaded = sem("x_loaded")
        bn_done = sem("bn_stats_done")
        mv_done = sem("mean_var_done")
        ve_done = sem("var_eps_done")
        rstd_done = sem("rstd_done")
        xn_ready = sem("xn_ready")
        t_ready = sem("xnT_in_psum")
        xb_ready = sem("xnT_bf16_written")
        xh_ready = sem("xnT_hi_written")
        xl_ready = sem("xnT_lo_written")
        qk_ready = sem("qk_in_psum")
        qh_ready = sem("qk_hi_written")
        ql_ready = sem("qk_lo_written")
        qh_copied = sem("qk_hi_copied")
        ql_copied = sem("qk_lo_copied")
        stack_loaded = [sem(f"stack{g}_loaded") for g in range(G)]
        max_loaded = [sem(f"max{g}_in_stack") for g in range(G)]
        s_ready = sem("scores_in_psum")
        max_done = sem("chunk_max_done")
        mh_done = sem("max_hi_done")
        mp_ready = sem("max_parts_ready")
        mt_ready = sem("max_T_in_psum")
        mts_ready = sem("max_T_written")
        st_ready = sem("scoresT_in_psum")
        exp_done = sem("exp_done")
        mask_done = sem("probs_masked")
        pv_done = sem("pv_done")
        ot_ready = sem("out_T_written")
        ot_stored = [sem(f"out_T{i}_regrouped") for i in range(2)]
        den_loaded = [sem(f"denominators{i}_regrouped") for i in range(2)]
        rc_ready = sem("denominators_inverted")
        rc_stored = sem("inverses_stored")
        rb_loaded = sem("inverses_spread")
        div_done = sem("attn_divided")
        ah_ready = sem("attn_hi_written")
        al_ready = sem("attn_lo_written")
        v_ready = sem("v_in_psum")
        va_ready = sem("v_written")
        qt_done = sem("quant_t_done")
        qz_done = sem("quant_over_done")
        qk_magic = sem("quant_guard_done")
        qe_done = sem("quant_exponent_done")
        qm_done = sem("quant_magic_done")
        qr_done = sem("quant_rounded")
        xq_ready = sem("xq_ready")
        ff_ready = sem("ffn_in_psum")
        y1_ready = sem("y1_written")
        y2_ready = sem("y2_written")
        xp_ready = sem("x_plus_bias")
        xy_ready = sem("x_plus_ffn")
        pj_ready = sem("proj_in_psum")
        out_ready = sem("out_written")
        out_stored = sem("out_stored")
        def qk_part(m, part, copy):
            pair = 2 * part + copy if m % 2 == 0 else part + 2 * copy
            return QKP[:, m // 2, pair, m % 2, :]

        def misc_of(kind, i):
            return MBS[MISC_BANK[kind, i]]

        def wait_alone(eng, always, *pairs):
            held = [(s, v if isinstance(v, int) else eng.compute_val(v)) for s, v in pairs]
            eng.wait_ge(*always)
            for s, v in held:
                eng.wait_ge(s, v)

        recips = nc.dram_tensor("recips", (H, T), F32, kind="Internal").ap()

        def attn_row(b):
            return AS[:, bass.ds(b % 2, 1), :, :].rearrange("p o a n -> p (o a) n")

        def x_slot(b):
            return X[:, bass.ds(b % 4, 1), :, :].rearrange("p o t c -> p (o t) c")

        block = ctx.enter_context(nc.Block())

        @block.sync
        def _(sp):
            def load_x(b):
                sp.dma_start(x_slot(b), x[bass.ds(b, 1), :, :].rearrange("o (t p) c -> p (o t) c", p=P)) \
                    .then_inc(x_loaded, 16)

            def load_stack(b, g):
                for h in range(HU):
                    r = 64 * (g % 2) + HD * h
                    for a in range(2):
                        sp.dma_start(STK[0:64, g, a, h, :].bitcast(F32),
                                     QKP[r:r + HD, g // 2, :, a, :].bitcast(F32)).then_inc(stack_loaded[g], 16)

            def load_max(b, g):
                sp.wait_ge(mts_ready, 4 * b + g + 1)
                sp.dma_start(STK[K_SCORE:K_ALL, g, 0, :, :].rearrange("p h n -> p (h n)").bitcast(F32),
                             MTS[:, g % 2, :].bitcast(F32)).then_inc(max_loaded[g], 16)

            def regroup(b, g, early):
                if g == 0 and not early:
                    wait_alone(sp, (w_loaded, 16), (al_ready, b), (rc_ready, b), (ot_ready, 4 * b + g + 1))
                else:
                    sp.wait_ge(ot_ready, 4 * b + g + 1)
                for i in range(HU):
                    r = 64 * (g % 2) + HD * i
                    sp.dma_start(attn_row(b)[r:r + HD, g // 2, :],
                                 OT[32 * i:32 * i + HD, g % 2, :]).then_inc(ot_stored[g % 2], 16)
                sp.dma_start(DEN[32 * g:32 * g + 32, :], OT[HD:P:32, g % 2, :]).then_inc(den_loaded[g % 2], 16)

            def store_recips(b):
                wait_alone(sp, (w_loaded, 16), (rc_ready, b + 1), (rb_loaded, 32 * (b + 1)))
                sp.dma_start(recips.rearrange("h (e j) -> (h e) j", e=8), RDEN[:, :]).then_inc(rc_stored, 16)

            def spread_recips(b, last):
                if not last:
                    wait_alone(sp, (w_loaded, 16), (rc_stored, 16 * (b + 1)), (t_ready, 2 * (b + 3)))
                else:
                    sp.wait_ge(rc_stored, 16 * (b + 1))
                    sp.wait_ge(qm_done, B)
                    sp.wait_ge(div_done, b)
                for ct in range(CT):
                    src = recips[8 * ct:8 * ct + 8, :].unsqueeze(1).broadcast_to([8, HD, T])
                    sp.dma_start(RB[:, ct, :], src).then_inc(rb_loaded, 16)

            sp.sem_inc(out_stored, 16)
            sp.sem_inc(rb_loaded, 32)
            load_x(0)
            sp.dma_start(w_raw, w_qkv.rearrange("(m p) c -> p m c", p=P)).then_inc(w_loaded, 16)
            sp.dma_start(BQ[:, :], b_qkv[0:2 * C].rearrange("(m p) -> p m", p=P),
                         allow_slow_non_contiguous=True).then_inc(small_loaded, 16)
            sp.dma_start(SC[:, 0:1], s_in.partition_broadcast(P)).then_inc(small_loaded, 16)
            sp.dma_start(SC[:, 1:2], s_k.partition_broadcast(P)).then_inc(small_loaded, 16)
            sp.dma_start(BV[:, :], b_qkv[2 * C:3 * C].partition_broadcast(P)).then_inc(small_loaded, 16)
            sp.dma_start(BP[:, :], b_proj.partition_broadcast(P)).then_inc(small_loaded, 16)
            sp.dma_start(BF[:, :], ffn_b.partition_broadcast(P)).then_inc(small_loaded, 16)
            sp.dma_start(wp_raw, w_proj.rearrange("(m p) c -> p m c", p=P)).then_inc(small_loaded, 16)
            sp.dma_start(kern_raw, ffn_w.rearrange("(m p) c -> p m c", p=P)).then_inc(small_loaded, 16)
            sp.wait_ge(x_loaded, 16)
            load_x(1)

            def load_features(g):
                for h in range(HU * g, HU * g + HU):
                    r = 16 * (h % 8)
                    if g < 2:
                        sp.dma_start(STK[64:K_SCORE, g, 0, h % HU, :].bitcast(F32),
                                     fq_parts[r:r + 16, :, :].bitcast(F32)).then_inc(feat_loaded[g], 16)
                    sp.dma_start(STK[64:K_SCORE, g, 1, h % HU, :].bitcast(F32),
                                 fk_parts[h // 8][r:r + 16, :, :].bitcast(F32)).then_inc(feat_loaded[g], 16)

            sp.wait_ge(ones_made, 1)
            sp.wait_ge(feat_parts, 2)
            load_features(0)
            load_features(1)
            sp.wait_ge(qh_copied, 2)
            sp.wait_ge(ql_copied, 2)
            load_stack(0, 0)
            load_stack(0, 1)
            sp.wait_ge(feat_parts, 4)
            sp.wait_ge(consts_made, 7)
            load_features(2)
            load_max(0, 0)
            sp.wait_ge(qh_copied, 4)
            sp.wait_ge(ql_copied, 4)
            load_stack(0, 2)
            load_features(3)

            def body(b, first, last, load):
                if load:
                    if not first:
                        sp.wait_ge(out_stored, 16 * b)
                    else:
                        for g in (2, 3):
                            sp.wait_ge(feat_loaded[g], 16 * HU)
                    sp.wait_ge(x_loaded, 16 * (b + 2))
                    load_x(b + 2)
                if not first:
                    sp.wait_ge(st_ready, ROW * b)
                load_stack(b, 3)
                load_max(b, 1)
                if not first:
                    regroup(b - 1, 3, False)
                load_max(b, 2)
                regroup(b, 0, first)
                if not last:
                    wait_alone(sp, (w_loaded, 16), (st_ready, ROW * b + SLOTS),
                               (qh_copied, 4 * (b + 1) + 2), (ql_copied, 4 * (b + 1) + 2))
                    load_stack(b + 1, 0)
                if not first:
                    store_recips(b - 1)
                    spread_recips(b - 1, last)
                if not last:
                    sp.wait_ge(st_ready, ROW * b + 2 * SLOTS)
                    load_stack(b + 1, 1)
                load_max(b, 3)
                regroup(b, 1, first)
                if not last:
                    wait_alone(sp, (w_loaded, 16), (st_ready, ROW * b + 3 * SLOTS),
                               (qh_copied, 4 * (b + 1) + 4), (ql_copied, 4 * (b + 1) + 4))
                    load_stack(b + 1, 2)
                    load_max(b + 1, 0)
                regroup(b, 2, first)
                if not first:
                    sp.wait_ge(out_ready, 2 * (b + 1))
                    sp.dma_start(out[bass.ds(b - 1, 1), :, :].rearrange("o (t p) c -> p (o t) c", p=P),
                                 x_slot(b + 3)).then_inc(out_stored, 16)

            body(0, True, False, True)
            with sp.Fori(1, B - 2) as b:
                body(b, False, False, True)
            body(B - 2, False, False, False)
            body(B - 1, False, True, False)
            regroup(B - 1, 3, False)
            store_recips(B - 1)
            spread_recips(B - 1, True)
            sp.wait_ge(out_ready, 2 * (B + 1))
            sp.dma_start(out[B - 1:B, :, :].rearrange("o (t p) c -> p (o t) c", p=P), x_slot(B - 1)) \
                .then_inc(out_stored, 16)
            sp.wait_ge(out_stored, 16 * (B + 1))

        @block.tensor
        def _(pe):
            mm = nc.tensor.matmul
            bank_read = [None, None]

            def done(kind, i, b):
                return {"V": (va_ready, 2 * b + i + 1), "T": (xl_ready, 2 * b + i + 3),
                        "QK": (ql_ready, 4 * b + i + 5), "FF": (y1_ready, 2 * b + i + 1),
                        "PJ": (out_ready, 2 * b + i + 1), "MT": (mts_ready, 4 * b + i + 2)}[kind]

            def misc(kind, i, b):
                n = MISC_BANK[kind, i]
                if bank_read[n]:
                    pe.wait_ge(*bank_read[n])
                bank_read[n] = done(kind, i, b)
                return MBS[n]

            def split3(o, a, b_, n):
                (ah, al), (bh, bl) = a, b_
                for ct in range(CT):
                    for i, (l, r) in enumerate(((ah, bh), (ah, bl), (al, bh))):
                        last = mm(o, l(ct), r(ct), start=(ct == 0 and i == 0), stop=(ct == CT - 1 and i == 2))
                return last

            def job_T(b, ct):
                if ct == 0:
                    pe.wait_ge(xn_ready, b + 1)
                bank = misc("T", ct, b - 1)
                for t in range(TT):
                    last = nc.tensor.transpose(bank[:, P * t:P * t + P], XN[:, t, P * ct:P * ct + P], IDF[:, :])
                last.then_inc(t_ready, 1)

            def job_QK(b, m):
                col = P * [0, 2, 1, 3][m]
                if m == 0:
                    pe.wait_ge(xl_ready, 2 * (b + 1))
                bank = misc("QK", m, b - 1)
                split3(bank[:, :], (lambda ct: WH[:, ct, col:col + P], lambda ct: WL[:, ct, col:col + P]),
                       (lambda ct: XH[:, ct, :], lambda ct: XL[:, ct, :]), T).then_inc(qk_ready, 1)

            def by_tokens(bank, i, ah, al, bh, bl):
                for t in (2 * i, 2 * i + 1):
                    o = bank[:, C * (t % 2):C * (t % 2) + C]
                    last = split3(o, (lambda ct: ah[:, ct, P * t:P * t + P], lambda ct: al[:, ct, P * t:P * t + P]),
                                  (bh, bl), C)
                return last

            def job_V(b, i):
                by_tokens(misc("V", i, b), i, XH, XL, lambda ct: WH[:, ct, 2 * C:3 * C], lambda ct: WL[:, ct, 2 * C:3 * C]) \
                    .then_inc(v_ready, 1)

            def job_PJ(b, i):
                if i == 0:
                    pe.wait_ge(al_ready, b + 2)
                by_tokens(misc("PJ", i, b + 1), i, AH, AL, lambda ct: PH[:, ct, :], lambda ct: PL[:, ct, :]).then_inc(pj_ready, 1)

            def job_FF(b, i):
                if i == 0:
                    pe.wait_ge(xq_ready, b + 1)
                    pe.wait_ge(kq_made, 1)
                bank = misc("FF", i, b)
                for t in (2 * i, 2 * i + 1):
                    for ct in range(CT):
                        last = mm(bank[:, C * (t % 2):C * (t % 2) + C], XQ[:, ct, P * t:P * t + P], KQ[:, ct, :],
                                  start=(ct == 0), stop=(ct == CT - 1))
                last.then_inc(ff_ready, 1)

            def job_MT(b, g):
                pe.wait_ge(mp_ready, 4 * b + g + 1)
                bank = misc("MT", (g - 1) % G, b if g else b - 1)
                nc.tensor.transpose(bank[0:2 * HU * TT, 0:P], MP[:, g % 2, :, :].rearrange("p a b -> p (a b)"),
                                    IDF[:, :]).then_inc(mt_ready, 1)

            def scores(b, g, c, early=False):
                qt, h0, nh = CHUNK_PLAN[c]
                w = P * (qt + 1)
                n = CHUNKS * g + c
                if c == 0:
                    if isinstance(b, int) and b == 0:
                        pe.wait_ge(feat_loaded[g], 16 * (2 * HU if g < 2 else HU))
                    pe.wait_ge(stack_loaded[g], 128 * (b + 1))
                if n >= 3:
                    pe.wait_ge(max_done, ROW * b + n - 2)
                elif not early:
                    pe.wait_ge(max_done, ROW * b - [1, 0, 2][n])
                for i in range(nh):
                    h, o = h0 + i, w * i
                    mm(SB_[n % 3][:, o:o + w], STK[0:K_SCORE, g, 0, h, P * qt:P * qt + P],
                       STK[0:K_SCORE, g, 1, h, 0:w], start=True, stop=False)
                    last = mm(SB_[n % 3][:, o + w - P:o + w], CMT[:, :], IDB[:, :], start=False, stop=True)
                last.then_inc(s_ready, 1)

            def scores_T(b, g, k, first):
                j, h0, nh = SLOT_PLAN[k]
                w = WJ[j]
                if k == 0:
                    pe.wait_ge(max_loaded[g], 16 * (b + 1))
                if not (first and g == 0 and k < 2):
                    pe.wait_ge(exp_done, ROW * b + SLOTS * g + k - 1)
                bank = STB[(SLOTS * g + k) % 2]
                for i in range(nh):
                    h = h0 + i
                    last = mm(bank[:, w * i:w * i + w], STK[0:K_ALL, g, 1, h, P * j:P * j + P],
                              STK[0:K_ALL, g, 0, h, P * j:T], start=True, stop=True)
                last.then_inc(st_ready, 1)

            def pv(b, g, j, first):
                pe.wait_ge(mask_done, 16 * b + 4 * g + j + 1)
                if j == 0:
                    if g == 0:
                        pe.wait_ge(va_ready, 2 * (b + 1))
                    if not (first and g == 0):
                        pe.wait_ge(ot_ready, 4 * b + g)
                for i in range(HU):
                    last = mm(PVB[32 * i:32 * i + 32, P * j:T],
                              VA[:, j, HU * g + i, :, :].rearrange("p a d -> p (a d)"),
                              PJ[j][:, i, :], start=(j == 0), stop=(j == TT - 1))
                last.then_inc(pv_done, 1)

            pe.sem_inc(pj_ready, 2)
            pe.wait_ge(ident_steps, 3)
            pe.wait_ge(w_loaded, 16)
            for n in range(4):
                ct, half = n // 2, n % 2
                for m in range(3):
                    last = nc.tensor.transpose(w_banks[n][:, P * m:P * m + P],
                                               w_raw[:, 3 * half + m, P * ct:P * ct + P], IDF[:, :])
                last.then_inc(setup_T, 1)
            pe.wait_ge(small_loaded, 16 * 8)
            for ct in range(CT):
                for m in range(2):
                    last = nc.tensor.transpose(STB[ct][:, P * m:P * m + P], wp_raw[:, m, P * ct:P * ct + P], IDF[:, :])
                last.then_inc(setup_T, 1)
            for ct in range(CT):
                job_T(0, ct)
            pe.wait_ge(setup_lo, 6)
            for m in range(4):
                job_QK(0, m)
            pe.wait_ge(consts_made, 8)
            for c in range(CHUNKS):
                scores(0, 0, c, True)
            job_MT(0, 0)
            for c in range(CHUNKS):
                scores(0, 1, c, True)

            def body(b, first, last):
                if not first:
                    for n in range(2):
                        job = [x for x in ORDER if MISC_BANK[x] == n][-1]
                        bank_read[n] = done(*job, b - 1)
                for g in range(G):
                    nb, ng = (b, g + 2) if g < 2 else (b + 1, g - 2)
                    ahead = not (last and g >= 2)
                    for k in range(SLOTS):
                        scores_T(b, g, k, first)
                        pb, pg = (b, g - 1) if g else (b - 1, 3)
                        if ahead:
                            scores(nb, ng, k)
                        if k in PV_AT[2:] and not (first and g == 0):
                            pv(pb, pg, PV_AT.index(k), False)
                        if k in PV_AT[:2]:
                            pv(b, g, PV_AT.index(k), first)
                        for i in due(V_AT, g, k):
                            job_V(b, i)
                        if due(MT_AT, g, k) and not (last and g == 3):
                            job_MT(*((b, g + 1) if g < 3 else (b + 1, 0)))
                        if not last:
                            for i in due(T_AT, g, k):
                                job_T(b + 1, i)
                            for i in due(QK_AT, g, k):
                                job_QK(b + 1, i)
                        for i in due(FF_AT, g, k):
                            job_FF(b, i)
                        if not first:
                            for i in due(PJ_AT, g, k):
                                job_PJ(b - 1, i)

            body(0, True, False)
            for n in range(2):
                pe.wait_ge(*bank_read[n])
            with pe.Fori(1, B - 1) as b:
                body(b, False, False)
            body(B - 1, False, True)
            for j in (2, 3):
                pv(B - 1, 3, j, False)
            for i in range(2):
                job_PJ(B - 1, i)

        @block.scalar
        def _(act):
            A = nc.scalar.activation

            act.dma_start(fq_raw, feat_q).then_inc(feat_raw, 16)
            act.dma_start(fk_raw, feat_k).then_inc(feat_raw, 16)
            act.dma_start(POS[:, :], pos.rearrange("a b -> (a b)").rearrange("(p o) -> p o", o=1)) \
                .then_inc(feat_raw, 16)

            def T_evac(b, ct):
                act.wait_ge(t_ready, 2 * b + ct + 1)
                bank = misc_of("T", ct)
                A(XB[:, ct, :], bank[:, :], ACT.Copy).then_inc(xb_ready, 1)
                A(XH[:, ct, :], bank[:, :], ACT.Copy).then_inc(xh_ready, 1)

            def QK_evac(b, m, first):
                act.wait_ge(qk_ready, 4 * b + m + 1)
                if not first:
                    for g in ((0, 1) if m < 2 else (2, 3)):
                        act.wait_ge(stack_loaded[g], 128 * b)
                bias = [0, 2, 1, 3][m]
                A(qk_part(m, 0, 0), misc_of("QK", m)[:, :], ACT.Identity, bias=BQ[:, bias:bias + 1]).then_inc(qh_ready, 1)

            def QK_copy_lo(b, m):
                act.wait_ge(ql_ready, 4 * b + m + 1)
                A(qk_part(m, 1, 1), qk_part(m, 1, 0).bitcast(F32), ACT.Copy).then_inc(ql_copied, 1)

            for n in range(4):
                ct, half = n // 2, n % 2
                act.wait_ge(setup_T, n + 1)
                src = w_banks[n][:, 0:3 * P]
                if half == 0:
                    A(WH[:, ct, 0:C], src[:, 0:C], ACT.Copy, scale=HD ** -0.5)
                    A(WH[:, ct, C:3 * P], src[:, C:3 * P], ACT.Copy).then_inc(setup_hi, 1)
                else:
                    A(WH[:, ct, 3 * P:3 * C], src, ACT.Copy).then_inc(setup_hi, 1)
            for ct in range(CT):
                act.wait_ge(setup_T, 5 + ct)
                A(PH[:, ct, :], STB[ct][:, 0:C], ACT.Copy).then_inc(setup_hi, 1)
            for ct in range(CT):
                T_evac(0, ct)
            act.wait_ge(setup_step, 6)
            for m in range(4):
                QK_evac(0, m, True)
                QK_copy_lo(0, m)

            def out_T(b, g, skip_wait):
                act.wait_ge(pv_done, 16 * b + 4 * g + 4)
                if not skip_wait:
                    act.wait_ge(ot_stored[g % 2], 64 * (2 * b + g // 2))
                    act.wait_ge(den_loaded[g % 2], 16 * (2 * b + g // 2))
                A(OT[:, g % 2, :], PVB[:, :], ACT.Copy).then_inc(ot_ready, 1)

            def attn_hi(b, ct):
                if ct == 0:
                    act.wait_ge(div_done, b + 1)
                    act.wait_ge(pj_ready, 2 * (b + 1))
                A(AH[:, ct, :], attn_row(b)[:, ct, :], ACT.Copy).then_inc(ah_ready, 1)

            def body(b, first, last):
                for g in range(G):
                    for k in range(SLOTS):
                        j, h0, nh = SLOT_PLAN[k]
                        act.wait_ge(st_ready, ROW * b + SLOTS * g + k + 1)
                        if k in (0, 4, 8, 10) and not (first and g == 0):
                            act.wait_ge(pv_done, 16 * b + 4 * g + j - 3)
                        A(PJ[j][:, h0:h0 + nh, :], STB[(SLOTS * g + k) % 2][:, 0:nh * WJ[j]]
                          .rearrange("p (h n) -> p h n", h=nh), ACT.Exp).then_inc(exp_done, 1)
                        pb, pg = (b, g - 1) if g else (b - 1, 3)
                        if not (first and g == 0):
                            if k == OUT_AT:
                                out_T(pb, pg, first and pg < 2)
                        if not last:
                            for i in due(T_AT, g, k, ACT_LAG["T"]):
                                if i == 0 and not first:
                                    act.wait_ge(xy_ready, b)
                                T_evac(b + 1, i)
                            for i in due(QK_AT, g, k, ACT_LAG["QK"]):
                                QK_evac(b + 1, i, False)
                            for i in due(QK_AT, g, k, ACT_LAG["copy_lo"]):
                                QK_copy_lo(b + 1, i)
                        if not first:
                            for ct in due(AH_AT, g, k):
                                attn_hi(b - 1, ct)
                        for i in due(FF_AT, g, k, ACT_LAG["FF"]):
                            act.wait_ge(ff_ready, 2 * b + i + 1)
                            if i == 0 and not last:
                                act.wait_ge(qz_done, b + 2)
                            A(Y1[:, 2 * i:2 * i + 2, :], misc_of("FF", i)[:, :].rearrange("p (t c) -> p t c", c=C),
                              ACT.Identity, scale=SC[:, 3:4]).then_inc(y1_ready, 1)

            body(0, True, False)
            with act.Fori(1, B - 1) as b:
                body(b, False, False)
            body(B - 1, False, True)
            out_T(B - 1, 3, False)
            for ct in range(CT):
                attn_hi(B - 1, ct)

        @block.vector
        def _(dve):
            V = nc.vector

            def stats(b):
                dve.wait_ge(x_loaded, 16 * (b + 1))
                for t in range(TT):
                    V.bn_stats(ST6[:, t, :], x_slot(b)[:, t, :]).then_inc(bn_done, 1)
                for t in range(TT):
                    wait_alone(dve, (x_loaded, 16), (bn_done, 4 * b + t + 1))
                    V.bn_aggr(MV[:, t, :], ST6[:, t, :]).then_inc(mv_done, 1)
                dve.wait_ge(mv_done, 4 * b + 4)
                V.tensor_scalar(VE[:, :], MV[:, :, 1], EPS, None, ALU.add).then_inc(ve_done, 1)

            def normalise(b):
                dve.wait_ge(rstd_done, b + 1)
                dve.wait_ge(t_ready, 2 * b)
                dve.wait_ge(qm_done, b)
                for t in range(TT):
                    ins = V.tensor_scalar(XN[:, t, :], x_slot(b)[:, t, :], MV[:, t, 0:1], RSTD[:, t:t + 1],
                                          ALU.subtract, ALU.mult)
                ins.then_inc(xn_ready, 1)

            def T_lo(b, ct):
                dve.wait_ge(xh_ready, 2 * b + ct + 1)
                V.tensor_tensor(XL[:, ct, :], misc_of("T", ct)[:, :], XH[:, ct, :].bitcast(F32), ALU.subtract) \
                    .then_inc(xl_ready, 1)

            def QK_lo(b, m):
                bias = [0, 2, 1, 3][m]
                dve.wait_ge(qh_ready, 4 * b + m + 1)
                V.scalar_tensor_tensor(out=qk_part(m, 1, 0), in0=misc_of("QK", m)[:, :], scalar=BQ[:, bias:bias + 1],
                                       in1=qk_part(m, 0, 0).bitcast(F32), op0=ALU.add, op1=ALU.subtract) \
                    .then_inc(ql_ready, 1)

            def QK_copy_hi(b, m):
                dve.wait_ge(qh_ready, 4 * b + m + 1)
                V.tensor_copy(qk_part(m, 0, 1), qk_part(m, 0, 0).bitcast(F32)).then_inc(qh_copied, 1)

            def chunk_max(b, g, c):
                qt, h0, nh = CHUNK_PLAN[c]
                n = CHUNKS * g + c
                dve.wait_ge(s_ready, ROW * b + n + 1)
                V.tensor_reduce(MX[:, g % 2, h0:h0 + nh, qt],
                                SB_[n % 3][:, 0:nh * P * (qt + 1)].rearrange("p (h w) -> p h w", h=nh),
                                AX_X, ALU.max, negate=True).then_inc(max_done, 1)

            def max_parts(b, g):
                p = g % 2
                mx = MX[:, p, :, :].rearrange("p h t -> p (h t)")
                dve.wait_ge(max_done, ROW * b + SLOTS * (g + 1))
                V.tensor_copy(MP[:, p, 0, :].bitcast(F32R), mx).then_inc(mh_done, 1)
                dve.wait_ge(mh_done, 4 * b + g + 1)
                V.tensor_tensor(MP[:, p, 1, :], mx, MP[:, p, 0, :], ALU.subtract).then_inc(mp_ready, 1)

            def max_T(b, g):
                dve.wait_ge(mt_ready, 4 * b + g + 1)
                V.tensor_copy(MTS[:, g % 2, :], misc_of("MT", (g - 1) % G)[0:2 * HU * TT, 0:P]).then_inc(mts_ready, 1)

            def v_evac(b, i, first):
                dve.wait_ge(v_ready, 2 * b + i + 1)
                if i == 0 and not first:
                    dve.wait_ge(pv_done, 16 * b)
                V.tensor_tensor(VA[:, 2 * i:2 * i + 2, :, 0, :],
                                misc_of("V", i)[:, :].rearrange("p (t h d) -> p t h d", h=H, d=HD),
                                BV[:, :].rearrange("p (h d) -> p h d", d=HD).unsqueeze(1).broadcast_to([P, 2, H, HD]),
                                ALU.add).then_inc(va_ready, 1)

            def invert(b):
                for i in range(2):
                    dve.wait_ge(den_loaded[i], 32 * (b + 1))
                V.reciprocal(RDEN[:, :], DEN[:, :]).then_inc(rc_ready, 1)

            def divide(b):
                dve.wait_ge(rb_loaded, 32 * (b + 2))
                for i in range(2):
                    dve.wait_ge(ot_stored[i], 128 * (b + 1))
                V.tensor_tensor(attn_row(b), attn_row(b), RB, ALU.mult).then_inc(div_done, 1)

            def result(b, i):
                dve.wait_ge(pj_ready, 2 * b + i + 3)
                dve.wait_ge(xy_ready, b + 1)
                xs = x_slot(b + 4)[:, 2 * i:2 * i + 2, :]
                V.tensor_tensor(xs, misc_of("PJ", i)[:, :].rearrange("p (t c) -> p t c", c=C), xs, ALU.add) \
                    .then_inc(out_ready, 1)

            def quant_magic(b):
                if isinstance(b, int) and b < 2:
                    dve.wait_ge(qk_magic, b + 1)
                else:
                    wait_alone(dve, (x_loaded, 16), (qk_magic, b + 1), (div_done, b - 1))
                V.tensor_scalar(QE.bitcast(I32), QT.bitcast(I32), 0x7F800000, None, ALU.bitwise_and) \
                    .then_inc(qe_done, 1)
                dve.wait_ge(qe_done, b + 1)
                V.scalar_tensor_tensor(out=QM, in0=QE, scalar=E4_LEAST, in1=QM, op0=ALU.max, op1=ALU.mult) \
                    .then_inc(qm_done, 1)

            step = [0]

            def then(ins):
                step[0] += 1
                ins.then_inc(setup_step, 1)
                dve.wait_ge(setup_step, step[0])

            dve.sem_inc(out_ready, 2)
            V.memset(STK[96:P, 0:2, 1, :, :].bitcast(F32), 1.0).then_inc(ones_made, 1)
            stats(0)
            dve.wait_ge(feat_raw, 48)
            for raw, parts, order in ((fq_raw, fq_parts, (0, 1, 2)), (fk_raw, fk_parts[0], (0, 2, 1))):
                V.tensor_copy(parts[:, order[1], :], raw)
                then(V.tensor_copy(parts[:, order[0], :], raw))
                V.tensor_tensor(parts[:, order[2], :], raw, parts[:, order[0], :].bitcast(F32), ALU.subtract) \
                    .then_inc(feat_parts, 1)
            dve.wait_ge(rstd_done, 1)
            for t in range(TT):
                ins = V.tensor_scalar(XN[:, t, :], x_slot(0)[:, t, :], MV[:, t, 0:1], RSTD[:, t:t + 1],
                                      ALU.subtract, ALU.mult)
            ins.then_inc(xn_ready, 1)
            dve.wait_ge(small_loaded, 16 * 8)
            then(V.tensor_scalar(BQ[:, 0:2], BQ[:, 0:2], HD ** -0.5, None, ALU.mult))
            then(V.reciprocal(SC[:, 4:5], SC[:, 1:2]))
            then(V.reciprocal(SC[:, 2:3], SC[:, 0:1]))
            then(V.tensor_tensor(SC[:, 3:4], SC[:, 0:1], SC[:, 1:2], ALU.mult))
            for n in range(4):
                ct, half = n // 2, n % 2
                src = w_banks[n][:, 0:3 * P]
                dve.wait_ge(setup_hi, n + 1)
                if half == 0:
                    V.scalar_tensor_tensor(out=WL[:, ct, 0:C], in0=src[:, 0:C], scalar=HD ** -0.5,
                                           in1=WH[:, ct, 0:C].bitcast(F32), op0=ALU.mult, op1=ALU.subtract)
                    V.tensor_tensor(WL[:, ct, C:3 * P], src[:, C:3 * P], WH[:, ct, C:3 * P].bitcast(F32),
                                    ALU.subtract).then_inc(setup_lo, 1)
                else:
                    V.tensor_tensor(WL[:, ct, 3 * P:3 * C], src, WH[:, ct, 3 * P:3 * C].bitcast(F32),
                                    ALU.subtract).then_inc(setup_lo, 1)
            for ct in range(CT):
                dve.wait_ge(setup_hi, 5 + ct)
                V.tensor_tensor(PL[:, ct, :], STB[ct][:, 0:C], PH[:, ct, :].bitcast(F32), ALU.subtract) \
                    .then_inc(setup_lo, 1)
            for ct in range(CT):
                T_lo(0, ct)
            for m in (0, 1):
                QK_lo(0, m)
                QK_copy_hi(0, m)
            pos_rows = POS[:, 0:1].broadcast_to([P, T])
            V.memset(fk_parts[1][:, 2, :].bitcast(F32), 0.0).then_inc(feat_parts, 1)
            then(V.tensor_copy(fk_parts[1][:, 0, :], pos_rows))
            V.tensor_tensor(fk_parts[1][:, 1, :], pos_rows, fk_parts[1][:, 0, :].bitcast(F32), ALU.subtract) \
                .then_inc(feat_parts, 1)
            for m in (2, 3):
                QK_lo(0, m)
                QK_copy_hi(0, m)
            for c in range(CHUNKS):
                chunk_max(0, 0, c)
            max_parts(0, 0)
            max_T(0, 0)
            dve.wait_ge(kq_step, 3)
            V.tensor_scalar(ke.bitcast(I32), kt.bitcast(I32), 0x7F800000, None, ALU.bitwise_and).then_inc(kq_step, 1)
            dve.wait_ge(kq_step, 4)
            V.scalar_tensor_tensor(out=km, in0=ke, scalar=E4_LEAST, in1=km, op0=ALU.max, op1=ALU.mult) \
                .then_inc(kq_step, 1)
            stats(1)
            for c in range(CHUNKS):
                chunk_max(0, 1, c)
            max_parts(0, 1)
            quant_magic(0)
            normalise(1)

            def body(b, first, last, more):
                for g in range(G):
                    nb, ng = (b, g + 2) if g < 2 else (b + 1, g - 2)
                    ahead = not (last and g >= 2)
                    for k in range(SLOTS):
                        if ahead:
                            chunk_max(nb, ng, k)
                        for i in due(V_AT, g, k, DVE_LAG["V"]):
                            v_evac(b, i, first)
                        for i in due(MT_AT, g, k, DVE_LAG["MT"]):
                            if not (last and i == 3):
                                max_T(*((b, i + 1) if i < 3 else (b + 1, 0)))
                        if not last:
                            for i in due(T_AT, g, k, DVE_LAG["T"]):
                                T_lo(b + 1, i)
                            for i in due(QK_AT, g, k, DVE_LAG["QK"]):
                                QK_lo(b + 1, i)
                            for i in due(QK_AT, g, k, DVE_LAG["copy_hi"]):
                                QK_copy_hi(b + 1, i)
                        if not first:
                            for i in due(PJ_AT, g, k, DVE_LAG["PJ"]):
                                result(b - 1, i)
                        if (g, k) == INVERT_AT and not first:
                            invert(b - 1)
                        if (g, k) == DIVIDE_AT and not first:
                            divide(b - 1)
                        if (g, k) == STATS_AT and more:
                            stats(b + 2)
                        if (g, k) == MAGIC_AT and not last:
                            quant_magic(b + 1)
                        if (g, k) == NORM_AT and more:
                            normalise(b + 2)
                    if ahead:
                        max_parts(nb, ng)

            body(0, True, False, True)
            with dve.Fori(1, B - 2) as b:
                body(b, False, False, True)
            body(B - 2, False, False, False)
            body(B - 1, False, True, False)
            invert(B - 1)
            divide(B - 1)
            dve.wait_ge(ah_ready, 2 * B)
            V.tensor_tensor(AL[:, :, :], attn_row(B - 1), AH[:, :, :].bitcast(F32), ALU.subtract) \
                .then_inc(al_ready, 1)
            for i in range(2):
                result(B - 1, i)

        @block.gpsimd
        def _(pool):
            GP = nc.gpsimd

            def rstd(b):
                pool.wait_ge(ve_done, b + 1)
                GP.tensor_tensor(RSTD[:, :], VE[:, :], NH[:, :], ALU.pow).then_inc(rstd_done, 1)

            def quant_scale(b):
                wait_alone(pool, (ident_steps, 3), (xb_ready, 2 * (b + 1)))
                GP.tensor_scalar(QT, XB[:, :, :], SC[:, 2:3], 1.0, ALU.mult, ALU.mult).then_inc(qt_done, 1)
                GP.tensor_scalar(QM, XB[:, :, :], SC[:, 2:3], E4_OVER, ALU.mult, ALU.mult).then_inc(qz_done, 1)
                wait_alone(pool, (ident_steps, 3), (qz_done, b + 1))
                GP.tensor_scalar(QM, QM, 0.0, E4_MAGIC, ALU.mult, ALU.add).then_inc(qk_magic, 1)

            def quant_round(b):
                pool.wait_ge(qm_done, b + 1)
                GP.tensor_tensor(QT, QT, QM, ALU.add).then_inc(qr_done, 1)

            def quant_write(b):
                pool.wait_ge(qr_done, b + 1)
                pool.wait_ge(ff_ready, 2 * b)
                GP.tensor_tensor(XQ[:, :, :], QT, QM, ALU.subtract).then_inc(xq_ready, 1)

            def mask(b, g, j):
                wait_alone(pool, (ident_steps, 3), (exp_done, ROW * b + SLOTS * g + LAST_SLOT[j] + 1))
                d = PJ[j][:, :, 0:P]
                GP.affine_select(out=d, in_=d, compare_op=ALU.is_ge, fill=0.0, base=0,
                                 pattern=[[0, HU], [1, P]], channel_multiplier=-1).then_inc(mask_done, 1)

            def ffn_bias(b):
                pool.wait_ge(y1_ready, 2 * (b + 1))
                GP.tensor_tensor(Y1[:, :, :], Y1[:, :, :], BF[:, :].unsqueeze(1).broadcast_to([P, TT, C]),
                                 ALU.add).then_inc(y2_ready, 1)

            def add_ffn(b):
                pool.wait_ge(y2_ready, b + 1)
                pool.wait_ge(xp_ready, b + 1)
                xs = x_slot(b + 4)
                GP.tensor_tensor(xs, xs, Y1[:, :, :], ALU.add).then_inc(xy_ready, 1)

            def add_bias(b):
                pool.wait_ge(xn_ready, b + 1)
                xs = x_slot(b)
                GP.tensor_tensor(xs, xs, BP[:, :].unsqueeze(1).broadcast_to([P, TT, C]), ALU.add) \
                    .then_inc(xp_ready, 1)

            def attn_parts(b):
                pool.wait_ge(ah_ready, 2 * (b + 1))
                GP.tensor_tensor(AL[:, :, :], attn_row(b), AH[:, :, :].bitcast(F32), ALU.subtract) \
                    .then_inc(al_ready, 1)

            pool.sem_inc(al_ready, 1)
            GP.memset(IDF[:, :], 0.0).then_inc(ident_steps, 1)
            pool.wait_ge(ident_steps, 1)
            GP.affine_select(out=IDF[:, :], in_=IDF[:, :], compare_op=ALU.not_equal, fill=1.0, base=0,
                             pattern=[[-1, P]], channel_multiplier=1).then_inc(ident_steps, 2)
            GP.memset(IDB[:, :], 0.0).then_inc(consts_made, 1)
            GP.memset(CMT[:, :], 0.0).then_inc(consts_made, 1)
            pool.wait_ge(consts_made, 2)
            GP.affine_select(out=IDB[:, :], in_=IDB[:, :], compare_op=ALU.not_equal, fill=1.0, base=0,
                             pattern=[[-1, P]], channel_multiplier=1).then_inc(consts_made, 1)
            GP.affine_select(out=CMT[:, :], in_=CMT[:, :], compare_op=ALU.is_ge, fill=MASKED, base=0,
                             pattern=[[1, P]], channel_multiplier=-1).then_inc(consts_made, 1)
            GP.memset(NH[:, :], -0.5).then_inc(consts_made, 1)
            pool.wait_ge(consts_made, 5)
            GP.memset(STK[96:P, 2:4, 1, :, :].bitcast(F32), 1.0).then_inc(consts_made, 1)
            pool.wait_ge(consts_made, 6)
            rstd(0)
            pool.wait_ge(rstd_done, 1)
            GP.memset(STK[64:P, 2:4, 0, :, :].bitcast(F32), 1.0).then_inc(consts_made, 1)
            pool.wait_ge(consts_made, 7)
            GP.memset(VA[:, :, :, 1, :].rearrange("p t h d -> p (t h) d"), 1.0).then_inc(consts_made, 1)
            pool.wait_ge(setup_step, 6)
            kr = XQ[:, 0, :]
            GP.tensor_scalar(kt, kr, SC[:, 4:5], 1.0, ALU.mult, ALU.mult).then_inc(kq_step, 1)
            GP.tensor_scalar(km, kr, SC[:, 4:5], E4_OVER, ALU.mult, ALU.mult).then_inc(kq_step, 1)
            pool.wait_ge(kq_step, 2)
            GP.tensor_scalar(km, km, 0.0, E4_MAGIC, ALU.mult, ALU.add).then_inc(kq_step, 1)
            pool.wait_ge(kq_step, 5)
            GP.tensor_tensor(kt, kt, km, ALU.add).then_inc(kq_step, 1)
            pool.wait_ge(kq_step, 6)
            GP.tensor_tensor(KQ[:, :, :].rearrange("p a c -> p (a c)"), kt, km, ALU.subtract).then_inc(kq_made, 1)
            pool.wait_ge(kq_made, 1)
            quant_scale(0)
            rstd(1)
            quant_round(0)
            quant_write(0)

            def body(b, first, last, more):
                for g in range(G):
                    if g == 0 and not first:
                        ffn_bias(b - 1)
                        add_ffn(b - 1)
                    if g == 1 and not last:
                        quant_scale(b + 1)
                    if g == 3 and not last:
                        quant_round(b + 1)
                    if g == 3 and more:
                        rstd(b + 2)
                    mask(b, g, 0)
                    if g == 1:
                        add_bias(b)
                    if g == 2 and not first:
                        attn_parts(b - 1)
                    if g == 3 and not last:
                        quant_write(b + 1)
                    for j in (1, 2, 3):
                        mask(b, g, j)

            body(0, True, False, True)
            with pool.Fori(1, B - 2) as b:
                body(b, False, False, True)
            body(B - 2, False, False, False)
            body(B - 1, False, True, False)
            ffn_bias(B - 1)
            add_ffn(B - 1)

    return nc


_INS = ["L0_attn_x", "L0_attn_w_qkv", "L0_attn_b_qkv", "L0_attn_w_proj", "L0_attn_b_proj",
        "L0_attn_pos_independent", "L0_ffn_kernel", "L0_ffn_input_scale", "L0_ffn_kernel_scale", "L0_ffn_bias"]


def kernel(**inputs):
    import numpy as _np
    import concourse.bacc as _bacc
    from concourse import mybir as _mybir
    from concourse.bass_utils import run_bass_kernel_spmd as _run

    nc = _bacc.Bacc("TRN2", target_bir_lowering=False, num_devices=1)
    arrays, args = {}, []

    def give(name, a):
        arrays[name] = a
        args.append(nc.dram_tensor(name, a.shape, _mybir.dt.from_np(a.dtype), kind="ExternalInput").ap())

    for name in _INS:
        give(f"in_{name}", _np.ascontiguousarray(inputs[name]))
    for name, table in zip(("feature_q", "feature_k"), position_tables()):
        give(name, table)
    args.append(nc.dram_tensor("out", (B, T, C), F32, kind="ExternalOutput").ap())
    build(nc, *args)
    r = _run(nc, [arrays], core_ids=[0])
    return r.results[0]["out"]
```
